# Optimizing a Trainium2 kernel written in Bass

```python
import numpy as np
import jax
import jax.numpy as jnp

def _softmax(x, axis=-1):
    return jax.nn.softmax(x, axis=axis)

def _gelu(x):
    return jax.nn.gelu(x, approximate=True)

def _silu(x):
    return jax.nn.silu(x)

def _sigmoid(x):
    return jax.nn.sigmoid(x)

def _layernorm(x, axis=-1, eps=1e-05):
    m = jnp.mean(x, axis=axis, keepdims=True)
    v = jnp.var(x, axis=axis, keepdims=True)
    return (x - m) / jnp.sqrt(v + eps)

def _scatter_add(tgt, idx, src, axis=0):
    return tgt.at[idx].add(src)

def _segment_sum(src, seg, n):
    return jax.ops.segment_sum(src, seg, n)
kernel_name = 'mk_adj_ffn_d4_adj_r2_44c171'

def setup_inputs(seed: int=0):
    np.random.seed(seed)
    _w = jnp.asarray

    def _rec_inputs():
        import jax
        import jax.numpy as jnp
        _gk = jax.random.key(seed)
        x = -0.0005207 + 1.001 * jax.random.normal(jax.random.fold_in(_gk, 1), (4096, 128), jnp.float32)
        _w = (1.0 + jnp.arange(4096, dtype=jnp.float32)) ** (-0.5)
        _w = _w / _w.mean()
        _pij = jnp.clip(0.000488281 * _w[:, None] * _w[None, :], 0.0, 1.0)
        _a = jax.random.uniform(jax.random.fold_in(_gk, 2), (4096, 4096)) < _pij
        _a = jnp.logical_or(_a, jnp.eye(4096, dtype=bool))
        _af = _a.astype(jnp.float32)
        _af = _af * jax.random.uniform(jax.random.fold_in(_gk, 3), (4096, 4096), jnp.float32, 0.05, 1)
        adj = _af
        return (x, adj)
    x, adj = _rec_inputs()

    def _L0_gnn_setup():
        import jax, jax.numpy as jnp
        import numpy as np
        D_IN = 128
        D_ATTN = 64
        STEPS = 2
        TOP_P = 0.9
        TAU = 1.0
        LN_EPS = 1e-05
        N_NODES = 4096

        def _top_p_attention(X, W1, W2, W3):
            q = X @ W1.T @ W2.T
            k = X @ W3.T
            logits = q @ k.T / TAU
            probs = jax.nn.softmax(logits, axis=-1)
            idx = jnp.argsort(-probs, axis=-1)
            sp = jnp.take_along_axis(probs, idx, axis=-1)
            cs = jnp.cumsum(sp, axis=-1)
            keep_sorted = cs - sp < TOP_P
            rows = jnp.arange(probs.shape[0])[:, None]
            mask = jnp.zeros(probs.shape, dtype=bool).at[rows, idx].set(keep_sorted)
            A = probs * mask
            return A / jnp.maximum(A.sum(-1, keepdims=True), 1e-12)
        key = jax.random.key(seed)
        ks = jax.random.split(key, 8)
        N, d, da, steps = (N_NODES, D_IN, D_ATTN, STEPS)
        X = jax.random.normal(ks[0], (N, d), dtype=jnp.float32)
        S = jax.random.uniform(ks[1], (N, N), dtype=jnp.float32)
        W1 = jax.random.normal(ks[2], (da, d), dtype=jnp.float32) / np.sqrt(d)
        W2 = jax.random.normal(ks[3], (da, da), dtype=jnp.float32) / np.sqrt(da)
        W3 = jax.random.normal(ks[4], (da, d), dtype=jnp.float32) / np.sqrt(d)
        U1 = jax.random.normal(ks[5], (steps, d, d), dtype=jnp.float32) / np.sqrt(d)
        U2 = jax.random.normal(ks[6], (steps, d, d), dtype=jnp.float32) / np.sqrt(d)
        ln_g = jnp.ones((d,), dtype=jnp.float32)
        ln_b = jnp.zeros((d,), dtype=jnp.float32)
        return {'X': X, 'S': S, 'W1': W1, 'W2': W2, 'W3': W3, 'U1': U1, 'U2': U2, 'ln_g': ln_g, 'ln_b': ln_b}
    _L0_gnn_all = _L0_gnn_setup()
    _L0_gnn_in = {k: v for k, v in _L0_gnn_all.items() if k in ('W1', 'W2', 'W3', 'U1', 'U2', 'ln_g', 'ln_b')}
    del _L0_gnn_all

    def _L0_ffn_setup():
        import jax, jax.numpy as jnp
        import numpy as np
        IN_CH = 128
        OUT_CH = 128
        key = jax.random.key(seed)
        kx, kw, kb = jax.random.split(key, 3)
        x = jax.random.normal(kx, (8, 2048, IN_CH), dtype=jnp.float32)
        bound = 1.0 / np.sqrt(IN_CH)
        weight = jax.random.uniform(kw, (OUT_CH, IN_CH), dtype=jnp.float32, minval=-bound, maxval=bound)
        bias = jax.random.uniform(kb, (OUT_CH,), dtype=jnp.float32, minval=-bound, maxval=bound)
        return {'x': x, 'weight': weight, 'bias': bias}
    _L0_ffn_all = _L0_ffn_setup()
    _L0_ffn_in = {k: v for k, v in _L0_ffn_all.items() if k in ('weight', 'bias')}
    del _L0_ffn_all

    def _L1_gnn_setup():
        import jax, jax.numpy as jnp
        import numpy as np
        N = 4096
        D = 128
        OUT = 128
        AVG_DEG = 32
        key = jax.random.key(seed)
        k1, k2, k3, k4, k5 = jax.random.split(key, 5)
        node_features = jax.random.normal(k1, (N, D), dtype=jnp.float32)
        edge_features = jax.random.normal(k2, (N, N), dtype=jnp.float32)
        u = jax.random.uniform(k3, (N, N), dtype=jnp.float32)
        adj = jnp.where(u < AVG_DEG / N, 1.0, 0.0).astype(jnp.float32)
        stdv = 1.0 / np.sqrt(OUT)
        weight = jax.random.uniform(k4, (2 * D + 1, OUT), minval=-stdv, maxval=stdv, dtype=jnp.float32)
        bias = jax.random.uniform(k5, (OUT,), minval=-stdv, maxval=stdv, dtype=jnp.float32)
        return {'node_features': node_features, 'edge_features': edge_features, 'adj': adj, 'weight': weight, 'bias': bias}
    _L1_gnn_all = _L1_gnn_setup()
    _L1_gnn_in = {k: v for k, v in _L1_gnn_all.items() if k in ('weight', 'bias')}
    del _L1_gnn_all

    def _L1_ffn_setup():
        import jax, jax.numpy as jnp
        import numpy as np
        B, T, C = (64, 192, 128)
        NH, NKV = (4, 2)
        HD = C // NH
        NREP = NH // NKV
        NE, TOPK = (8, 2)
        HID = int(8 / 3 * C)
        EPS_RMS = 1e-06

        def _rope_tables(t_len):
            inv_freq = 1.0 / 10000.0 ** (np.arange(0, HD, 2, dtype=np.float32) / HD)
            t = np.arange(t_len, dtype=np.float32)
            freqs = np.outer(t, inv_freq)
            emb = np.concatenate([freqs, freqs], axis=-1)
            return (jnp.asarray(np.cos(emb)), jnp.asarray(np.sin(emb)))

        def _rotate_half(x):
            h = x.shape[-1] // 2
            return jnp.concatenate([-x[..., h:], x[..., :h]], axis=-1)

        def _rmsnorm(v, w):
            return v * jax.lax.rsqrt(jnp.mean(v * v, axis=-1, keepdims=True) + EPS_RMS) * w
        key = jax.random.key(seed)
        ks = jax.random.split(key, 10)
        s = lambda k, shape: jax.random.normal(k, shape, jnp.float32) * 0.02
        return {'x': jax.random.normal(ks[0], (B, T, C), jnp.float32), 'ln1_w': jnp.ones((C,), jnp.float32), 'ln2_w': jnp.ones((C,), jnp.float32), 'wq': s(ks[1], (NH * HD, C)), 'wk': s(ks[2], (NKV * HD, C)), 'wv': s(ks[3], (NKV * HD, C)), 'wo': s(ks[4], (C, C)), 'router_w': s(ks[5], (NE, C)), 'w1': s(ks[6], (NE, HID, C)), 'w2': s(ks[7], (NE, C, HID)), 'w3': s(ks[8], (NE, HID, C))}
    _L1_ffn_all = _L1_ffn_setup()
    _L1_ffn_in = {k: v for k, v in _L1_ffn_all.items() if k in ('ln1_w', 'ln2_w', 'wq', 'wk', 'wv', 'wo', 'router_w', 'w1', 'w2', 'w3')}
    del _L1_ffn_all

    def _L2_gnn_setup():
        import jax, jax.numpy as jnp
        import numpy as np
        from jax import lax
        D_MODEL = 128
        D_STATE = 16
        D_CONV = 4
        EXPAND = 2
        D_INNER = EXPAND * D_MODEL
        DT_RANK = (D_MODEL + 15) // 16
        N = 2048
        EPS = 1e-05

        def _mamba(h, w_in, conv_w, conv_b, w_xp, w_dt, b_dt, A_log, D_skip, w_out):
            L = h.shape[0]
            xz = h @ w_in
            xc, z = (xz[:, :D_INNER], xz[:, D_INNER:])
            xpad = jnp.pad(xc, ((D_CONV - 1, 0), (0, 0)))
            xconv = sum((xpad[k:k + L] * conv_w[:, k] for k in range(D_CONV))) + conv_b
            u = jax.nn.silu(xconv)
            dbc = u @ w_xp
            dt = jax.nn.softplus(dbc[:, :DT_RANK] @ w_dt + b_dt)
            B = dbc[:, DT_RANK:DT_RANK + D_STATE]
            C = dbc[:, DT_RANK + D_STATE:]
            A = -jnp.exp(A_log)
            dA = jnp.exp(dt[:, :, None] * A[None])
            dBu = dt[:, :, None] * B[:, None, :] * u[:, :, None]

            def step(hst, inp):
                dAt, dBut, Ct = inp
                hst = dAt * hst + dBut
                return (hst, hst @ Ct)
            _, ys = lax.scan(step, jnp.zeros((D_INNER, D_STATE), h.dtype), (dA, dBu, C))
            y = ys + u * D_skip
            y = y * jax.nn.silu(z)
            return y @ w_out
        key = jax.random.key(seed)
        ks = jax.random.split(key, 16)
        x = jax.random.normal(ks[0], (N, D_MODEL), dtype=jnp.float32)
        a = jax.random.uniform(ks[1], (N, N), dtype=jnp.float32)
        adj = a / a.sum(axis=1, keepdims=True)
        s = lambda fi, fo: 1.0 / np.sqrt(fi)
        gcn_w = jax.random.uniform(ks[2], (D_MODEL, D_MODEL), jnp.float32, -s(D_MODEL, 0), s(D_MODEL, 0))
        gcn_b = jnp.zeros((D_MODEL,), jnp.float32)
        ln_g = jnp.ones((D_MODEL,), jnp.float32)
        ln_b = jnp.zeros((D_MODEL,), jnp.float32)
        w_in = jax.random.normal(ks[3], (D_MODEL, 2 * D_INNER), jnp.float32) * s(D_MODEL, 0)
        conv_w = jax.random.normal(ks[4], (D_INNER, D_CONV), jnp.float32) * s(D_CONV, 0)
        conv_b = jnp.zeros((D_INNER,), jnp.float32)
        w_xp = jax.random.normal(ks[5], (D_INNER, DT_RANK + 2 * D_STATE), jnp.float32) * s(D_INNER, 0)
        w_dt = jax.random.normal(ks[6], (DT_RANK, D_INNER), jnp.float32) * s(DT_RANK, 0)
        b_dt = jnp.log(jnp.expm1(jnp.exp(jax.random.uniform(ks[7], (D_INNER,), jnp.float32, np.log(0.001), np.log(0.1)))))
        A_log = jnp.log(jnp.broadcast_to(jnp.arange(1, D_STATE + 1, dtype=jnp.float32), (D_INNER, D_STATE)))
        D_skip = jnp.ones((D_INNER,), jnp.float32)
        w_out = jax.random.normal(ks[8], (D_INNER, D_MODEL), jnp.float32) * s(D_INNER, 0)
        return dict(x=x, adj=adj, gcn_w=gcn_w, gcn_b=gcn_b, ln_g=ln_g, ln_b=ln_b, w_in=w_in, conv_w=conv_w, conv_b=conv_b, w_xp=w_xp, w_dt=w_dt, b_dt=b_dt, A_log=A_log, D_skip=D_skip, w_out=w_out)
    _L2_gnn_all = _L2_gnn_setup()
    _L2_gnn_in = {k: v for k, v in _L2_gnn_all.items() if k in ('gcn_w', 'gcn_b', 'ln_g', 'ln_b', 'w_in', 'conv_w', 'conv_b', 'w_xp', 'w_dt', 'b_dt', 'A_log', 'D_skip', 'w_out')}
    del _L2_gnn_all

    def _L2_ffn_setup():
        import jax, jax.numpy as jnp
        import numpy as np
        C = 128
        HID = 512
        E = 8
        TEMP = 1.0
        key = jax.random.key(seed)
        ks = jax.random.split(key, 7)
        x = jax.random.normal(ks[0], (8, 8192, C), dtype=jnp.float32)
        W1 = jax.random.normal(ks[1], (C, HID), dtype=jnp.float32) * 0.02
        b1 = jnp.zeros((HID,), dtype=jnp.float32)
        Wg = jax.random.normal(ks[2], (HID, E), dtype=jnp.float32) * 0.02
        bg = jnp.zeros((E,), dtype=jnp.float32)
        Wd = jax.random.normal(ks[3], (E, HID, C), dtype=jnp.float32) * 0.02
        bd = jnp.zeros((E, C), dtype=jnp.float32)
        return {'x': x, 'W1': W1, 'b1': b1, 'Wg': Wg, 'bg': bg, 'Wd': Wd, 'bd': bd}
    _L2_ffn_all = _L2_ffn_setup()
    _L2_ffn_in = {k: v for k, v in _L2_ffn_all.items() if k in ('W1', 'b1', 'Wg', 'bg', 'Wd', 'bd')}
    del _L2_ffn_all

    def _L3_gnn_setup():
        import jax, jax.numpy as jnp
        import numpy as np
        N = 4096
        C = 128
        key = jax.random.key(seed)
        k1, k2, k3 = jax.random.split(key, 3)
        x = jax.random.normal(k1, (N, C), dtype=jnp.float32)
        evals = jax.random.uniform(k2, (N,), dtype=jnp.float32)
        evecs = jax.random.normal(k3, (N, N), dtype=jnp.float32)
        t = jnp.ones((1,), dtype=jnp.float32)
        return {'x': x, 'evals': evals, 'evecs': evecs, 't': t}
    _L3_gnn_all = _L3_gnn_setup()
    _L3_gnn_in = {k: v for k, v in _L3_gnn_all.items() if k in ('evals', 't')}
    del _L3_gnn_all

    def _L3_ffn_setup():
        import jax, jax.numpy as jnp
        import numpy as np
        D_MODEL = 128
        EXPERT_DIM = 256
        NUM_EXPERTS = 8
        TOP_K = 2
        SEQ_LEN = 1024
        BATCH = 2
        key = jax.random.key(seed)
        ks = jax.random.split(key, 8)
        s = 0.02
        x = jax.random.normal(ks[0], (SEQ_LEN, BATCH, D_MODEL), dtype=jnp.float32)
        Wg = jax.random.normal(ks[1], (D_MODEL, NUM_EXPERTS), dtype=jnp.float32) * s
        bg = jax.random.normal(ks[2], (NUM_EXPERTS,), dtype=jnp.float32) * s
        bias = jnp.zeros((NUM_EXPERTS,), dtype=jnp.float32)
        W1 = jax.random.normal(ks[3], (NUM_EXPERTS, D_MODEL, EXPERT_DIM), dtype=jnp.float32) * s
        b1 = jax.random.normal(ks[4], (NUM_EXPERTS, EXPERT_DIM), dtype=jnp.float32) * s
        W2 = jax.random.normal(ks[5], (NUM_EXPERTS, EXPERT_DIM, D_MODEL), dtype=jnp.float32) * s
        b2 = jax.random.normal(ks[6], (NUM_EXPERTS, D_MODEL), dtype=jnp.float32) * s
        return {'x': x, 'Wg': Wg, 'bg': bg, 'bias': bias, 'W1': W1, 'b1': b1, 'W2': W2, 'b2': b2}
    _L3_ffn_all = _L3_ffn_setup()
    _L3_ffn_in = {k: v for k, v in _L3_ffn_all.items() if k in ('Wg', 'bg', 'bias', 'W1', 'b1', 'W2', 'b2')}
    del _L3_ffn_all
    return {'x': x, 'adj': adj, 'L0_gnn_W1': _L0_gnn_in['W1'], 'L0_gnn_W2': _L0_gnn_in['W2'], 'L0_gnn_W3': _L0_gnn_in['W3'], 'L0_gnn_U1': _L0_gnn_in['U1'], 'L0_gnn_U2': _L0_gnn_in['U2'], 'L0_gnn_ln_g': _L0_gnn_in['ln_g'], 'L0_gnn_ln_b': _L0_gnn_in['ln_b'], 'L0_ffn_weight': _L0_ffn_in['weight'], 'L0_ffn_bias': _L0_ffn_in['bias'], 'L1_gnn_weight': _L1_gnn_in['weight'], 'L1_gnn_bias': _L1_gnn_in['bias'], 'L1_ffn_ln1_w': _L1_ffn_in['ln1_w'], 'L1_ffn_ln2_w': _L1_ffn_in['ln2_w'], 'L1_ffn_wq': _L1_ffn_in['wq'], 'L1_ffn_wk': _L1_ffn_in['wk'], 'L1_ffn_wv': _L1_ffn_in['wv'], 'L1_ffn_wo': _L1_ffn_in['wo'], 'L1_ffn_router_w': _L1_ffn_in['router_w'], 'L1_ffn_w1': _L1_ffn_in['w1'], 'L1_ffn_w2': _L1_ffn_in['w2'], 'L1_ffn_w3': _L1_ffn_in['w3'], 'L2_gnn_gcn_w': _L2_gnn_in['gcn_w'], 'L2_gnn_gcn_b': _L2_gnn_in['gcn_b'], 'L2_gnn_ln_g': _L2_gnn_in['ln_g'], 'L2_gnn_ln_b': _L2_gnn_in['ln_b'], 'L2_gnn_w_in': _L2_gnn_in['w_in'], 'L2_gnn_conv_w': _L2_gnn_in['conv_w'], 'L2_gnn_conv_b': _L2_gnn_in['conv_b'], 'L2_gnn_w_xp': _L2_gnn_in['w_xp'], 'L2_gnn_w_dt': _L2_gnn_in['w_dt'], 'L2_gnn_b_dt': _L2_gnn_in['b_dt'], 'L2_gnn_A_log': _L2_gnn_in['A_log'], 'L2_gnn_D_skip': _L2_gnn_in['D_skip'], 'L2_gnn_w_out': _L2_gnn_in['w_out'], 'L2_ffn_W1': _L2_ffn_in['W1'], 'L2_ffn_b1': _L2_ffn_in['b1'], 'L2_ffn_Wg': _L2_ffn_in['Wg'], 'L2_ffn_bg': _L2_ffn_in['bg'], 'L2_ffn_Wd': _L2_ffn_in['Wd'], 'L2_ffn_bd': _L2_ffn_in['bd'], 'L3_gnn_evals': _L3_gnn_in['evals'], 'L3_gnn_t': _L3_gnn_in['t'], 'L3_ffn_Wg': _L3_ffn_in['Wg'], 'L3_ffn_bg': _L3_ffn_in['bg'], 'L3_ffn_bias': _L3_ffn_in['bias'], 'L3_ffn_W1': _L3_ffn_in['W1'], 'L3_ffn_b1': _L3_ffn_in['b1'], 'L3_ffn_W2': _L3_ffn_in['W2'], 'L3_ffn_b2': _L3_ffn_in['b2']}

def reference(x, adj, L0_gnn_W1, L0_gnn_W2, L0_gnn_W3, L0_gnn_U1, L0_gnn_U2, L0_gnn_ln_g, L0_gnn_ln_b, L0_ffn_weight, L0_ffn_bias, L1_gnn_weight, L1_gnn_bias, L1_ffn_ln1_w, L1_ffn_ln2_w, L1_ffn_wq, L1_ffn_wk, L1_ffn_wv, L1_ffn_wo, L1_ffn_router_w, L1_ffn_w1, L1_ffn_w2, L1_ffn_w3, L2_gnn_gcn_w, L2_gnn_gcn_b, L2_gnn_ln_g, L2_gnn_ln_b, L2_gnn_w_in, L2_gnn_conv_w, L2_gnn_conv_b, L2_gnn_w_xp, L2_gnn_w_dt, L2_gnn_b_dt, L2_gnn_A_log, L2_gnn_D_skip, L2_gnn_w_out, L2_ffn_W1, L2_ffn_b1, L2_ffn_Wg, L2_ffn_bg, L2_ffn_Wd, L2_ffn_bd, L3_gnn_evals, L3_gnn_t, L3_ffn_Wg, L3_ffn_bg, L3_ffn_bias, L3_ffn_W1, L3_ffn_b1, L3_ffn_W2, L3_ffn_b2):
    import jax
    import jax.numpy as jnp

    def _L0_gnn_ref(X, S, W1, W2, W3, U1, U2, ln_g, ln_b):
        import jax, jax.numpy as jnp
        import numpy as np
        D_IN = 128
        D_ATTN = 64
        STEPS = 2
        TOP_P = 0.9
        TAU = 1.0
        LN_EPS = 1e-05
        N_NODES = 4096

        def _top_p_attention(X, W1, W2, W3):
            q = X @ W1.T @ W2.T
            k = X @ W3.T
            logits = q @ k.T / TAU
            probs = jax.nn.softmax(logits, axis=-1)
            idx = jnp.argsort(-probs, axis=-1)
            sp = jnp.take_along_axis(probs, idx, axis=-1)
            cs = jnp.cumsum(sp, axis=-1)
            keep_sorted = cs - sp < TOP_P
            rows = jnp.arange(probs.shape[0])[:, None]
            mask = jnp.zeros(probs.shape, dtype=bool).at[rows, idx].set(keep_sorted)
            A = probs * mask
            return A / jnp.maximum(A.sum(-1, keepdims=True), 1e-12)
        N = X.shape[0]
        R = S + jnp.eye(N, dtype=X.dtype)
        R = R / R.sum(-1, keepdims=True)
        Z = jnp.zeros_like(X)
        Xf = X
        Xa = X
        for n in range(STEPS):
            A = _top_p_attention(Xa, W1, W2, W3)
            Xf = R @ Xf
            Xa = A @ Xa
            Z = Z + Xf @ U1[n].T + Xa @ U2[n].T
        h = X + Z
        mu = h.mean(-1, keepdims=True)
        var = jnp.mean((h - mu) ** 2, axis=-1, keepdims=True)
        return (h - mu) / jnp.sqrt(var + LN_EPS) * ln_g + ln_b

    def _L0_ffn_ref(x, weight, bias):
        import jax, jax.numpy as jnp
        import numpy as np
        IN_CH = 128
        OUT_CH = 128
        return jnp.einsum('bsi,oi->bso', x, weight) + bias

    def _L1_gnn_ref(node_features, edge_features, adj, weight, bias):
        import jax, jax.numpy as jnp
        import numpy as np
        N = 4096
        D = 128
        OUT = 128
        AVG_DEG = 32
        neighbor_node_features = adj @ node_features
        neighbor_edge_features = jnp.einsum('ij,ji->i', adj, edge_features)[:, None]
        support = jnp.concatenate((node_features, neighbor_node_features, neighbor_edge_features), axis=1)
        return support @ weight + bias

    def _L1_ffn_ref(x, ln1_w, ln2_w, wq, wk, wv, wo, router_w, w1, w2, w3):
        import jax, jax.numpy as jnp
        import numpy as np
        B, T, C = (64, 192, 128)
        NH, NKV = (4, 2)
        HD = C // NH
        NREP = NH // NKV
        NE, TOPK = (8, 2)
        HID = int(8 / 3 * C)
        EPS_RMS = 1e-06

        def _rope_tables(t_len):
            inv_freq = 1.0 / 10000.0 ** (np.arange(0, HD, 2, dtype=np.float32) / HD)
            t = np.arange(t_len, dtype=np.float32)
            freqs = np.outer(t, inv_freq)
            emb = np.concatenate([freqs, freqs], axis=-1)
            return (jnp.asarray(np.cos(emb)), jnp.asarray(np.sin(emb)))

        def _rotate_half(x):
            h = x.shape[-1] // 2
            return jnp.concatenate([-x[..., h:], x[..., :h]], axis=-1)

        def _rmsnorm(v, w):
            return v * jax.lax.rsqrt(jnp.mean(v * v, axis=-1, keepdims=True) + EPS_RMS) * w
        Bx, Tx, Cx = x.shape
        h = _rmsnorm(x, ln1_w)
        q = (h @ wq.T).reshape(Bx, Tx, NH, HD).transpose(0, 2, 1, 3)
        k = (h @ wk.T).reshape(Bx, Tx, NKV, HD).transpose(0, 2, 1, 3)
        v = (h @ wv.T).reshape(Bx, Tx, NKV, HD).transpose(0, 2, 1, 3)
        cos, sin = _rope_tables(Tx)
        cos, sin = (cos[None, None], sin[None, None])
        q = q * cos + _rotate_half(q) * sin
        k = k * cos + _rotate_half(k) * sin
        k = jnp.repeat(k, NREP, axis=1)
        v = jnp.repeat(v, NREP, axis=1)
        scores = jnp.einsum('bhtd,bhsd->bhts', q, k) / jnp.sqrt(jnp.float32(HD))
        causal = jnp.tril(jnp.ones((Tx, Tx), dtype=bool))
        scores = jnp.where(causal[None, None], scores, jnp.float32(-1e+30))
        att = jax.nn.softmax(scores, axis=-1)
        y = jnp.einsum('bhts,bhsd->bhtd', att, v).transpose(0, 2, 1, 3).reshape(Bx, Tx, Cx)
        x = x + y @ wo.T
        flat = _rmsnorm(x, ln2_w).reshape(-1, Cx)
        probs = jax.nn.softmax(flat @ router_w.T, axis=-1)
        tp, ti = jax.lax.top_k(probs, TOPK)
        tp = tp / (jnp.sum(tp, axis=-1, keepdims=True) + 1e-09)
        weights = jnp.sum(tp[..., None] * jax.nn.one_hot(ti, NE, dtype=flat.dtype), axis=1)
        out = jnp.zeros_like(flat)
        for e in range(NE):
            hh = jax.nn.silu(flat @ w1[e].T) * (flat @ w3[e].T)
            out = out + weights[:, e:e + 1] * (hh @ w2[e].T)
        return x + out.reshape(Bx, Tx, Cx)

    def _L2_gnn_ref(x, adj, gcn_w, gcn_b, ln_g, ln_b, w_in, conv_w, conv_b, w_xp, w_dt, b_dt, A_log, D_skip, w_out):
        import jax, jax.numpy as jnp
        import numpy as np
        from jax import lax
        D_MODEL = 128
        D_STATE = 16
        D_CONV = 4
        EXPAND = 2
        D_INNER = EXPAND * D_MODEL
        DT_RANK = (D_MODEL + 15) // 16
        N = 2048
        EPS = 1e-05

        def _mamba(h, w_in, conv_w, conv_b, w_xp, w_dt, b_dt, A_log, D_skip, w_out):
            L = h.shape[0]
            xz = h @ w_in
            xc, z = (xz[:, :D_INNER], xz[:, D_INNER:])
            xpad = jnp.pad(xc, ((D_CONV - 1, 0), (0, 0)))
            xconv = sum((xpad[k:k + L] * conv_w[:, k] for k in range(D_CONV))) + conv_b
            u = jax.nn.silu(xconv)
            dbc = u @ w_xp
            dt = jax.nn.softplus(dbc[:, :DT_RANK] @ w_dt + b_dt)
            B = dbc[:, DT_RANK:DT_RANK + D_STATE]
            C = dbc[:, DT_RANK + D_STATE:]
            A = -jnp.exp(A_log)
            dA = jnp.exp(dt[:, :, None] * A[None])
            dBu = dt[:, :, None] * B[:, None, :] * u[:, :, None]

            def step(hst, inp):
                dAt, dBut, Ct = inp
                hst = dAt * hst + dBut
                return (hst, hst @ Ct)
            _, ys = lax.scan(step, jnp.zeros((D_INNER, D_STATE), h.dtype), (dA, dBu, C))
            y = ys + u * D_skip
            y = y * jax.nn.silu(z)
            return y @ w_out
        h = jax.nn.relu(adj @ x @ gcn_w + gcn_b)
        mu = h.mean(-1, keepdims=True)
        var = h.var(-1, keepdims=True)
        h = (h - mu) * lax.rsqrt(var + EPS) * ln_g + ln_b
        return _mamba(h, w_in, conv_w, conv_b, w_xp, w_dt, b_dt, A_log, D_skip, w_out)

    def _L2_ffn_ref(x, W1, b1, Wg, bg, Wd, bd):
        import jax, jax.numpy as jnp
        import numpy as np
        C = 128
        HID = 512
        E = 8
        TEMP = 1.0
        orig_shape = x.shape
        xf = x.reshape(-1, orig_shape[-1])
        H = jax.nn.gelu(xf @ W1 + b1, approximate=False)
        probs = jax.nn.softmax((H @ Wg + bg) / TEMP, axis=-1)
        assign = jnp.argmax(probs, axis=-1)
        out = jnp.zeros_like(xf)
        for e in range(Wd.shape[0]):
            y = H @ Wd[e] + bd[e]
            sel = (assign == e)[:, None]
            out = out + jnp.where(sel, probs[:, e:e + 1] * y, 0.0)
        return out.reshape(orig_shape)

    def _L3_gnn_ref(x, evals, evecs, t):
        import jax, jax.numpy as jnp
        import numpy as np
        N = 4096
        C = 128
        t_eff = jnp.clip(t[0], 1e-08, None)
        x_spec = jnp.einsum('nk,nc->kc', evecs, x)
        coefs = jnp.exp(-evals * t_eff)[:, None]
        out = jnp.einsum('nk,kc->nc', evecs, coefs * x_spec)
        return out

    def _L3_ffn_ref(x, Wg, bg, bias, W1, b1, W2, b2):
        import jax, jax.numpy as jnp
        import numpy as np
        D_MODEL = 128
        EXPERT_DIM = 256
        NUM_EXPERTS = 8
        TOP_K = 2
        SEQ_LEN = 1024
        BATCH = 2
        x_flat = x.reshape(-1, D_MODEL)
        gate_logits = x_flat @ Wg + bg + bias
        topk_vals, topk_idx = jax.lax.top_k(gate_logits, TOP_K)
        topk_w = jax.nn.softmax(topk_vals, axis=-1)
        combine = (jax.nn.one_hot(topk_idx, NUM_EXPERTS, dtype=x.dtype) * topk_w[..., None]).sum(axis=1)
        h = jax.nn.relu(jnp.einsum('td,edh->teh', x_flat, W1) + b1)
        y = jnp.einsum('teh,ehd->ted', h, W2) + b2
        out = jnp.einsum('ted,te->td', y, combine)
        return out.reshape(x.shape)
    x = x + _L0_gnn_ref(_layernorm(x, axis=-1), adj, L0_gnn_W1, L0_gnn_W2, L0_gnn_W3, L0_gnn_U1, L0_gnn_U2, L0_gnn_ln_g, L0_gnn_ln_b)
    x = x + _L0_ffn_ref(_layernorm(x, axis=-1)[None], L0_ffn_weight, L0_ffn_bias)[0]
    x = x + _L1_gnn_ref(_layernorm(x, axis=-1), adj, adj, L1_gnn_weight, L1_gnn_bias)
    x = x + _L1_ffn_ref(_layernorm(x, axis=-1)[None], L1_ffn_ln1_w, L1_ffn_ln2_w, L1_ffn_wq, L1_ffn_wk, L1_ffn_wv, L1_ffn_wo, L1_ffn_router_w, L1_ffn_w1, L1_ffn_w2, L1_ffn_w3)[0]
    x = x + _L2_gnn_ref(_layernorm(x, axis=-1), adj, L2_gnn_gcn_w, L2_gnn_gcn_b, L2_gnn_ln_g, L2_gnn_ln_b, L2_gnn_w_in, L2_gnn_conv_w, L2_gnn_conv_b, L2_gnn_w_xp, L2_gnn_w_dt, L2_gnn_b_dt, L2_gnn_A_log, L2_gnn_D_skip, L2_gnn_w_out)
    x = x + _L2_ffn_ref(_layernorm(x, axis=-1)[None], L2_ffn_W1, L2_ffn_b1, L2_ffn_Wg, L2_ffn_bg, L2_ffn_Wd, L2_ffn_bd)[0]
    x = x + _L3_gnn_ref(_layernorm(x, axis=-1), L3_gnn_evals, adj, L3_gnn_t)
    x = x + _L3_ffn_ref(_layernorm(x, axis=-1)[None], L3_ffn_Wg, L3_ffn_bg, L3_ffn_bias, L3_ffn_W1, L3_ffn_b1, L3_ffn_W2, L3_ffn_b2)[0]
    return x

_drawn_inputs = setup_inputs


def setup_inputs(seed=0):
    import zlib

    import numpy as np

    out = dict(_drawn_inputs(seed))
    spreads = {'L0_gnn_ln_g': (1.0, 0.2),
     'L0_gnn_ln_b': (0.0, 0.1),
     'L1_ffn_ln1_w': (1.0, 0.6),
     'L1_ffn_ln2_w': (1.0, 0.6),
     'L2_gnn_gcn_b': (0.0, 0.1),
     'L2_gnn_ln_g': (1.0, 0.563),
     'L2_gnn_ln_b': (0.0, 0.324),
     'L2_gnn_conv_b': (0.0, 0.425),
     'L2_gnn_D_skip': (1.0, 0.6),
     'L2_ffn_b1': (0.0, 2.0),
     'L2_ffn_bg': (0.0, 2.0),
     'L2_ffn_bd': (0.0, 2.0),
     'L3_ffn_bias': (0.0, 2.0)}
    factors = {'L1_ffn_wq': 8.0,
     'L1_ffn_wk': 8.0,
     'L1_ffn_wv': 8.0,
     'L1_ffn_wo': 8.0,
     'L1_ffn_router_w': 8.0,
     'L1_ffn_w1': 8.0,
     'L1_ffn_w2': 8.0,
     'L1_ffn_w3': 8.0,
     'L2_gnn_w_dt': 16.045,
     'L2_gnn_b_dt': 14.543,
     'L2_gnn_A_log': 10.293,
     'L2_ffn_W1': 46.261,
     'L2_ffn_Wg': 47.391,
     'L2_ffn_Wd': 45.176,
     'L3_ffn_Wg': 56.88,
     'L3_ffn_bg': 64.0,
     'L3_ffn_W1': 63.728,
     'L3_ffn_b1': 200.0,
     'L3_ffn_W2': 52.44,
     'L3_ffn_b2': 200.0,
     'L2_gnn_w_xp': 2.918,
     'L3_gnn_evals': 8.0}
    for name, (base, spread) in spreads.items():
        noise = np.random.default_rng([zlib.crc32(name.encode()), seed]).standard_normal(out[name].shape)
        drawn = base * np.exp(spread * noise) if base else spread * noise
        out[name] = jnp.asarray(drawn.astype(out[name].dtype))
    for name, factor in factors.items():
        out[name] = (out[name] * factor).astype(out[name].dtype)
    return out
```

```python
import concourse.bass as bass
from concourse import mybir
from contextlib import ExitStack
import numpy as np

F32 = mybir.dt.float32
ALU = mybir.AluOpType
ACT = mybir.ActivationFunctionType
AX = mybir.AxisListType

P = 128
N = 4096
C = 128
NT = N // P
CH = 512
NCH = N // CH
TPC = CH // P
NQ = 4
JT = NT // NQ


class Stage:

    def __init__(self, nc, name):
        self.nc, self.name, self.stack, self.sems = nc, name, ExitStack(), []

    def __enter__(self):
        return self

    def __exit__(self, *exc):
        if exc[0] is None:
            if self.sems:
                self.nc.clear_and_free_semaphores(self.sems)
                self.nc.all_engine_barrier()
        self.stack.close()

    def sb(self, name, shape, dt=F32):
        return self.stack.enter_context(self.nc.sbuf_tensor(f"{self.name}_{name}", shape, dt))

    def ps(self, name, shape, dt=F32):
        return self.stack.enter_context(self.nc.psum_tensor(f"{self.name}_{name}", shape, dt))

    def sem(self, name):
        s = self.nc.alloc_semaphore(f"{self.name}_{name}")
        self.sems.append(s)
        return s


class Chain:

    def __init__(self, eng, sem):
        self.eng, self.sem, self.base, self.k, self.turn, self.per = eng, sem, 0, 0, None, 0

    def step(self, instruction):
        self.eng.wait_ge(self.sem, self.later(instruction))

    def later(self, instruction):
        instruction.then_inc(self.sem, 1)
        self.k += 1
        at = self.base + self.k
        return at if self.turn is None else self.turn * self.per + at

    def loop(self, turn, per):
        self.base, self.k, self.turn, self.per = self.base + self.k, 0, turn, per

    def end(self, trips):
        assert self.k == self.per, (self.k, self.per)
        self.base, self.k, self.turn = self.base + self.per * trips, 0, None


def flat(ap):
    return ap.rearrange("p a b -> p (a b)")


def over(ap, n):
    return ap.unsqueeze(2).to_broadcast([ap.shape[0], ap.shape[1], n])



def load(nc, name, pairs):
    with Stage(nc, name) as st:
        loaded = [st.sem("loaded0"), st.sem("loaded1")]
        with nc.Block() as block:
            @block.sync
            def _(sp):
                for to, of in pairs[0::2]:
                    sp.dma_start(to, of).then_inc(loaded[0], 16)
                sp.wait_ge(loaded[0], 16 * len(pairs[0::2]))

            @block.scalar
            def _(act):
                for to, of in pairs[1::2]:
                    act.dma_start(to, of).then_inc(loaded[1], 16)
                if pairs[1::2]:
                    act.wait_ge(loaded[1], 16 * len(pairs[1::2]))


def make_identity(nc, ident, ones_row):
    with Stage(nc, "identity") as st:
        zeroed = st.sem("zeroed")
        with nc.Block() as block:
            @block.gpsimd
            def _(pool):
                pool.memset(ones_row, 1.0)
                pool.memset(ident, 0.0).then_inc(zeroed, 1)
                pool.wait_ge(zeroed, 1)
                pool.affine_select(out=ident, in_=ident, compare_op=ALU.not_equal, fill=1.0,
                                   base=0, pattern=[[-1, P]], channel_multiplier=1)



def norm(nc, name, x, xn, xT, ident, eps, center=True, gamma=None, beta=None):
    G = 4
    TG = NT // G
    with Stage(nc, name) as st:
        mean = st.sb("mean", [P, NT])
        var = st.sb("var", [P, NT])
        std = st.sb("std", [P, NT])
        sq = st.sb("sq", [P, NT, C])
        banks = [st.ps(f"bank{k}", [P, CH]) for k in range(NCH)] if xT is not None else []
        dve_step = st.sem("dve_step")
        var_ready = st.sem("var_ready")
        std_ready = st.sem("std_ready")
        xn_ready = st.sem("xn_ready")
        transposed = st.sem("transposed")
        with nc.Block() as block:
            @block.vector
            def _(dve):
                chain = Chain(dve, dve_step)
                for g in range(G):
                    s = slice(g * TG, (g + 1) * TG)
                    src = x[:, s, :]
                    if center:
                        chain.step(dve.tensor_reduce(mean[:, s], src, axis=AX.X, op=ALU.add))
                        chain.step(dve.tensor_scalar(mean[:, s], mean[:, s], 1.0 / C, None, ALU.mult))
                        chain.step(dve.tensor_tensor(xn[:, s, :], src, over(mean[:, s], C), ALU.subtract))
                        src = xn[:, s, :]
                    chain.step(dve.tensor_tensor(sq[:, s, :], src, src, ALU.mult))
                    chain.step(dve.tensor_reduce(var[:, s], sq[:, s, :], axis=AX.X, op=ALU.add))
                chain.step(dve.tensor_scalar(var[:, :], var[:, :], 1.0 / C, eps, ALU.mult, ALU.add))
                dve.tensor_copy(var[:, :], var[:, :]).then_inc(var_ready, 1)
                dve.wait_ge(std_ready, 1)
                chain.step(dve.reciprocal(std[:, :], std[:, :]))
                chain.step(dve.tensor_tensor(mean[:, :], std[:, :], std[:, :], ALU.mult))
                chain.step(dve.scalar_tensor_tensor(mean[:, :], mean[:, :], -0.5, var[:, :], ALU.mult, ALU.mult))
                chain.step(dve.scalar_tensor_tensor(std[:, :], mean[:, :], 1.5, std[:, :], ALU.add, ALU.mult))
                for g in range(G):
                    s = slice(g * TG, (g + 1) * TG)
                    src = xn[:, s, :] if center else x[:, s, :]
                    dve.tensor_tensor(xn[:, s, :], src, over(std[:, s], C), ALU.mult).then_inc(xn_ready, 1)

            @block.scalar
            def _(act):
                act.wait_ge(var_ready, 1)
                act.activation(std[:, :], var[:, :], ACT.Sqrt).then_inc(std_ready, 1)
                for k in range(len(banks)):
                    act.wait_ge(transposed, k + 1)
                    act.activation(xT[:, k * CH:(k + 1) * CH], banks[k][:, :], ACT.Identity,
                                   scale=gamma if gamma is not None else 1.0,
                                   bias=beta if beta is not None else 0.0)

            @block.tensor
            def _(pe):
                for k in range(len(banks)):
                    pe.wait_ge(xn_ready, k * TPC // TG + 1)
                    for j in range(TPC):
                        last = pe.transpose(banks[k][:, j * P:(j + 1) * P], xn[:, k * TPC + j, :], ident)
                    last.then_inc(transposed, 1)


def to_channels(nc, name, a, aT, ident):
    with Stage(nc, name) as st:
        banks = [st.ps(f"bank{k}", [P, CH]) for k in range(NCH)]
        transposed = st.sem("transposed")
        with nc.Block() as block:
            @block.tensor
            def _(pe):
                for k in range(NCH):
                    for j in range(TPC):
                        last = pe.transpose(banks[k][:, j * P:(j + 1) * P], a[:, k * TPC + j, :], ident)
                    last.then_inc(transposed, 1)

            @block.scalar
            def _(act):
                for k in range(0, NCH, 2):
                    act.wait_ge(transposed, k + 1)
                    act.activation(aT[:, k * CH:(k + 1) * CH], banks[k][:, :], ACT.Copy)

            @block.vector
            def _(dve):
                for k in range(1, NCH, 2):
                    dve.wait_ge(transposed, k + 1)
                    dve.tensor_copy(aT[:, k * CH:(k + 1) * CH], banks[k][:, :])


def to_nodes(nc, name, aT, ident, write):
    with Stage(nc, name) as st:
        banks = [st.ps(f"bank{k}", [P, CH]) for k in range(NCH)]
        transposed = st.sem("transposed")
        step = st.sem("step")
        with nc.Block() as block:
            @block.tensor
            def _(pe):
                for k in range(NCH):
                    for j in range(TPC):
                        at = (k * TPC + j) * P
                        last = pe.transpose(banks[k][:, j * P:(j + 1) * P], aT[:, at:at + P], ident)
                    last.then_inc(transposed, 1)

            @block.vector
            def _(dve):
                chain = Chain(dve, step)
                for k in range(NCH):
                    dve.wait_ge(transposed, k + 1)
                    write(dve, chain, k, banks[k][:, :].rearrange("p (t c) -> p t c", c=C))



def project_T(nc, name, out, terms, func=ACT.Identity, bias=None):
    m = out.shape[0]
    with Stage(nc, name) as st:
        banks = [st.ps(f"bank{k}", [P, CH]) for k in range(NCH)]
        summed = st.sem("summed")
        with nc.Block() as block:
            @block.tensor
            def _(pe):
                for k in range(NCH):
                    for n, (lhsT, rhs) in enumerate(terms):
                        last = pe.matmul(banks[k][0:m, :], lhsT, rhs[:, k * CH:(k + 1) * CH],
                                         start=n == 0, stop=n == len(terms) - 1)
                    last.then_inc(summed, 1)

            @block.scalar
            def _(act):
                for k in range(NCH):
                    act.wait_ge(summed, k + 1)
                    act.activation(out[:, k * CH:(k + 1) * CH], banks[k][0:m, :], func,
                                   bias=bias if bias is not None else 0.0)


def project_add(nc, name, x, terms, ones_row, bias_row=None, extra=None):
    with Stage(nc, name) as st:
        banks = [st.ps(f"bank{k}", [P, CH]) for k in range(NCH)]
        summed = st.sem("summed")
        step = st.sem("step")
        with nc.Block() as block:
            @block.tensor
            def _(pe):
                for k in range(NCH):
                    for j in range(TPC):
                        at = (k * TPC + j) * P
                        rows = [(aT[:, at:at + P], w) for aT, w in terms]
                        if bias_row is not None:
                            rows.append((ones_row, bias_row))
                        for n, (lhsT, rhs) in enumerate(rows):
                            last = pe.matmul(banks[k][:, j * C:(j + 1) * C], lhsT, rhs,
                                             start=n == 0, stop=n == len(rows) - 1)
                    last.then_inc(summed, 1)

            @block.vector
            def _(dve):
                chain = Chain(dve, step)
                for k in range(NCH):
                    s = slice(k * TPC, (k + 1) * TPC)
                    dve.wait_ge(summed, k + 1)
                    chain.step(dve.tensor_tensor(flat(x[:, s, :]), flat(x[:, s, :]), banks[k][:, :], ALU.add))
                    if extra is not None:
                        extra(dve, chain, s)



def aggregate(nc, name, adj_d, a, outT):
    with Stage(nc, name) as st:
        slot = [st.sb(f"slot{q}", [P, JT, CH]) for q in range(NQ)]
        bank = [st.ps(f"bank{b}", [P, CH]) for b in range(2)]
        loaded = [st.sem(f"loaded{q}") for q in range(NQ)]
        used = [st.sem(f"used{q}") for q in range(NQ)]
        summed = [st.sem(f"summed{b}") for b in range(2)]
        taken = [st.sem(f"taken{b}") for b in range(2)]
        with nc.Block() as block:
            @block.sync
            def _(sp):
                for q in range(NQ):
                    sp.dma_start(flat(slot[q][:, :, :]), adj_d[0, q].rearrange("p t c -> p (t c)")).then_inc(loaded[q], 16)
                with sp.Fori(1, NCH) as i:
                    for q in range(NQ):
                        sp.wait_ge(used[q], i)
                        sp.dma_start(flat(slot[q][:, :, :]), adj_d[bass.ds(i, 1), q].rearrange("o p t c -> p (o t c)")).then_inc(loaded[q], 16)

            @block.tensor
            def _(pe):
                for b in range(2):
                    pe.sem_inc(taken[b], 1)
                with pe.Fori(0, NCH // 2) as i:
                    for b in range(2):
                        pe.wait_ge(taken[b], i + 1)
                        for q in range(NQ):
                            pe.wait_ge(loaded[q], i * 32 + 16 * (b + 1))
                            for t in range(JT):
                                last = pe.matmul(bank[b][:, :], a[:, q * JT + t, :], slot[q][:, t, :],
                                                 start=q == 0 and t == 0, stop=q == NQ - 1 and t == JT - 1)
                            last.then_inc(used[q], 1)
                        pe.drain().then_inc(summed[b], 1)

            @block.scalar
            def _(act):
                with act.Fori(0, NCH // 2) as i:
                    for b in range(2):
                        act.wait_ge(summed[b], i + 1)
                        act.activation(outT[:, bass.ds(i * (2 * CH) + b * CH, CH)], bank[b][:, :],
                                       ACT.Copy).then_inc(taken[b], 1)


def row_sums(nc, name, adj_n, adj_t, rowsum, edge):
    with Stage(nc, name) as st:
        a = [st.sb(f"a{q}", [P, NCH, CH]) for q in range(NQ)]
        b = [st.sb(f"b{q}", [P, NCH, CH]) for q in range(NQ)]
        part = st.sb("part", [P, NQ])
        parte = st.sb("parte", [P, NQ])
        loaded = [st.sem(f"loaded{q}") for q in range(NQ)]
        used = [st.sem(f"used{q}") for q in range(NQ)]
        summed = st.sem("summed")
        step = st.sem("step")
        with nc.Block() as block:
            @block.sync
            def _(sp):
                with sp.Fori(0, JT) as i:
                    for q in range(NQ):
                        sp.wait_ge(used[q], i + 1)
                        sp.dma_start(a[q][:, :, :], adj_n[:, q, :, bass.ds(i, 1), :]
                                     .rearrange("k p o c -> p (k o) c")).then_inc(loaded[q], 16)
                        sp.dma_start(b[q][:, :, :], adj_t[:, q, :, bass.ds(i, 1), :]
                                     .rearrange("k p o c -> p (k o) c")).then_inc(loaded[q], 16)

            @block.scalar
            def _(act):
                with act.Fori(0, JT) as i:
                    for q in range(NQ):
                        act.wait_ge(loaded[q], i * 32 + 32)
                        act.wait_ge(used[q], i + 1)
                        act.activation(flat(a[q][:, :, :]), flat(a[q][:, :, :]), ACT.Copy,
                                       accum_out=part[:, q:q + 1]).then_inc(summed, 1)

            @block.vector
            def _(dve):
                for q in range(NQ):
                    dve.sem_inc(used[q], 1)
                chain = Chain(dve, step)
                with dve.Fori(0, JT) as i:
                    chain.loop(i, NQ)
                    for q in range(NQ):
                        dve.wait_ge(summed, i * NQ + q + 1)
                        chain.step(dve.scalar_tensor_tensor(
                            flat(b[q][:, :, :]), flat(a[q][:, :, :]), 1.0, flat(b[q][:, :, :]),
                            ALU.mult, ALU.mult, accum_out=parte[:, q:q + 1]))
                        at = i + q * JT
                        dve.tensor_copy(edge[:, bass.ds(at, 1)], parte[:, q:q + 1])
                        dve.tensor_copy(rowsum[:, bass.ds(at, 1)], part[:, q:q + 1]).then_inc(used[q], 1)
                chain.end(JT)



def top_p_attention(nc, name, qT, kT, xa, out, ident):
    D = 64
    TOP_P = 0.9
    WIDTH = 12.0
    ROUNDS = 22
    with Stage(nc, name) as st:
        q = [st.sb(f"q{s}", [D, P]) for s in range(2)]
        logit = [st.sb(f"logit{s}", [P, N]) for s in range(2)]
        prob = [st.sb(f"prob{s}", [P, N]) for s in range(2)]
        probT = st.sb("probT", [P, N])
        small = st.sb("small", [P, 2, 11])
        MAGIC = 1.5 * 2 ** 21
        MAX, NEG, SUM, NEED, LO, STEP, TRIAL, MASS, KEPT, INV, HI = ([small[:, s, v:v + 1] for s in range(2)]
                                                                 for v in range(11))
        rest = st.sb("rest", [P, N])
        eighth = st.sb("eighth", [P, 2])
        run = st.sb("run", [P, N + 1])
        lg = st.ps("lg", [P, 2, 2 * CH])
        tr = [st.ps(f"tr{b}", [P, CH]) for b in range(2)]
        acc = [st.ps(f"acc{s}", [P, C]) for s in range(2)]
        q_ready = st.sem("q_ready")
        q_used = st.sem("q_used")
        lg_ready = st.sem("lg_ready")
        lg_taken = st.sem("lg_taken")
        neg_ready = st.sem("neg_ready")
        exp_ready = st.sem("exp_ready")
        kept_ready = st.sem("kept_ready")
        turned = st.sem("turned")
        turned_taken = st.sem("turned_taken")
        acc_ready = st.sem("acc_ready")
        acc_taken = st.sem("acc_taken")
        dve_step = st.sem("dve_step")
        round_step = st.sem("round_step")
        logit_free = st.sem("logit_free")

        with nc.Block() as block:
            def tiles(eng, before, each):
                if before:
                    before(0, 0)
                with eng.Fori(0, NT // 2 - 1) as i:
                    for s in range(2):
                        each(i * 2 + s, s, False)
                for s in range(2):
                    each(NT - 2 + s, s, s == 1)

            @block.gpsimd
            def _(pool):
                pool.sem_inc(q_used, 2)
                with pool.Fori(0, NT // 2) as i:
                    for s in range(2):
                        pool.wait_ge(q_used, i * 2 + s + 1)
                        pool.tensor_copy(q[s][:, :], qT[:, bass.ds(i * (2 * P) + s * P, P)]).then_inc(q_ready, 1)

            @block.tensor
            def _(pe):
                def logits(t, s):
                    pe.wait_ge(q_ready, t + 1)
                    for c in range(NCH):
                        if c % 2 == 0:
                            pe.wait_ge(lg_taken, t * 4 + c // 2 + 1)
                        last = pe.matmul(lg[:, c // 2 % 2, c % 2 * CH:(c % 2 + 1) * CH], q[s][:, :],
                                         kT[:, c * CH:(c + 1) * CH], start=True, stop=True)
                        if c % 2:
                            last.then_inc(lg_ready, 1)
                    pe.drain().then_inc(q_used, 1)

                def transpose4(t, s, g):
                    pe.wait_ge(turned_taken, t * NCH + g + 1)
                    for j in range(TPC):
                        at = (g * TPC + j) * P
                        last = pe.transpose(tr[g % 2][:, j * P:(j + 1) * P], prob[s][:, at:at + P], ident)
                    last.then_inc(turned, 1)

                def weigh(t, s):
                    pe.wait_ge(kept_ready, t + 1)
                    pe.wait_ge(acc_taken, t + 1)
                    transpose4(t, s, 0)
                    transpose4(t, s, 1)
                    for g in range(NCH):
                        pe.wait_ge(turned_taken, t * NCH + g + 3)
                        for j in range(TPC):
                            n = g * TPC + j
                            last = pe.matmul(acc[s][:, :], probT[:, n * P:(n + 1) * P], xa[:, n, :],
                                             start=n == 0, stop=n == NT - 1)
                        if g + 2 < NCH:
                            transpose4(t, s, g + 2)
                    last.then_inc(acc_ready, 1)

                pe.sem_inc(lg_taken, 2)
                pe.sem_inc(turned_taken, 2)
                pe.sem_inc(acc_taken, 2)

                def each(t, s, end):
                    if not end:
                        logits(t + 1, 1 - s)
                    weigh(t, s)
                tiles(pe, logits, each)

            @block.scalar
            def _(act):
                def exps(t, s):
                    act.wait_ge(logit_free, t + 1)
                    for h in range(4):
                        act.wait_ge(lg_ready, t * 4 + h + 1)
                        act.activation(logit[s][:, h * 1024:(h + 1) * 1024], lg[:, h % 2, :],
                                       ACT.Copy).then_inc(lg_taken, 1)
                    act.wait_ge(neg_ready, t + 1)
                    act.activation(prob[s][:, :], prob[s][:, :], ACT.Exp, bias=eighth[:, 0:1])
                    act.activation(rest[:, :], rest[:, :], ACT.Exp, bias=eighth[:, 1:2]).then_inc(exp_ready, 1)

                def turn(t, s):
                    act.wait_ge(acc_ready, t + 1)
                    for g in range(NCH):
                        act.wait_ge(turned, t * NCH + g + 1)
                        act.activation(probT[:, g * CH:(g + 1) * CH], tr[g % 2][:, :],
                                       ACT.Copy).then_inc(turned_taken, 1)

                act.sem_inc(logit_free, 2)
                act.sem_inc(acc_ready, 1)

                def each(t, s, end):
                    if not end:
                        exps(t + 1, 1 - s)
                    turn(t, s)
                tiles(act, exps, each)

            @block.vector
            def _(dve):
                chain = Chain(dve, dve_step)
                rounds = Chain(dve, round_step)

                def row_max(t, s):
                    dve.wait_ge(lg_taken, t * 4 + 6)
                    chain.step(dve.tensor_reduce(MAX[s], logit[s][:, :], axis=AX.X, op=ALU.max))
                    chain.step(dve.tensor_scalar(NEG[s], MAX[s], -1.0, -0.125, ALU.mult, ALU.add))
                    chain.step(dve.tensor_scalar(prob[s][:, :], logit[s][:, :], NEG[s], MAGIC, ALU.add, ALU.add))
                    chain.step(dve.tensor_scalar(prob[s][:, :], prob[s][:, :], -MAGIC, None, ALU.add))
                    chain.step(dve.scalar_tensor_tensor(rest[:, :], logit[s][:, :], MAX[s], prob[s][:, :],
                                                        ALU.subtract, ALU.subtract))
                    dve.sem_inc(neg_ready, 1)

                def threshold(t, s):
                    dve.wait_ge(exp_ready, t + 1)
                    chain.step(dve.scalar_tensor_tensor(prob[s][:, :], prob[s][:, :], 1.0, rest[:, :],
                                                        ALU.mult, ALU.mult, accum_out=SUM[s]))
                    chain.step(dve.tensor_scalar(NEED[s], SUM[s], TOP_P, None, ALU.mult))
                    chain.step(dve.tensor_scalar(LO[s], MAX[s], -WIDTH, None, ALU.add))
                    ready = chain.later(dve.memset(STEP[s], WIDTH / 2))
                    with dve.Fori(0, ROUNDS) as r:
                        rounds.loop(t * ROUNDS + r, 5)
                        dve.wait_ge(dve_step, ready)
                        rounds.step(dve.tensor_tensor(TRIAL[s], LO[s], STEP[s], ALU.add))
                        rounds.step(dve.scalar_tensor_tensor(
                            run[:, 0:N], logit[s][:, :], TRIAL[s], prob[s][:, :],
                            ALU.is_gt, ALU.mult, accum_out=MASS[s]))
                        rounds.step(dve.scalar_tensor_tensor(MASS[s], MASS[s], NEED[s], STEP[s],
                                                             ALU.is_ge, ALU.mult))
                        rounds.step(dve.tensor_tensor(LO[s], LO[s], MASS[s], ALU.add))
                        rounds.step(dve.tensor_scalar(STEP[s], STEP[s], 0.5, None, ALU.mult))
                    rounds.base, rounds.k = 0, 0
                    chain.step(dve.tensor_scalar(HI[s], LO[s], 2.0 ** -22, None, ALU.mult))
                    chain.step(dve.scalar_tensor_tensor(HI[s], LO[s], -2.0 ** -22, HI[s], ALU.mult, ALU.max))
                    chain.step(dve.scalar_tensor_tensor(HI[s], HI[s], WIDTH / 2 ** ROUNDS, LO[s], ALU.max, ALU.add))
                    k, g = prob[s][:, :], logit[s][:, :]
                    chain.step(dve.scalar_tensor_tensor(k, g, LO[s], k, ALU.is_gt, ALU.mult))
                    chain.step(dve.scalar_tensor_tensor(g, g, HI[s], k, ALU.is_gt, ALU.mult,
                                                        accum_out=run[:, 0:1]))
                    chain.step(dve.tensor_tensor_scan(run[:, 1:N + 1], k, g, run[:, 0:1], ALU.add, ALU.subtract))
                    chain.step(dve.scalar_tensor_tensor(k, run[:, 0:N], NEED[s], k, ALU.is_lt, ALU.mult))
                    chain.step(dve.scalar_tensor_tensor(k, g, 0.0, k, ALU.max, ALU.max, accum_out=KEPT[s]))
                    dve.sem_inc(kept_ready, 1)
                    dve.sem_inc(logit_free, 1)
                    chain.step(dve.scalar_tensor_tensor(KEPT[s], SUM[s], 1e-12, KEPT[s], ALU.mult, ALU.max))
                    chain.step(dve.reciprocal(INV[s], KEPT[s]))

                def scale(t, s):
                    dve.wait_ge(acc_ready, t + 2)
                    at = t * C
                    chain.step(dve.tensor_scalar(flat(out[:, :, :])[:, bass.ds(at, C)], acc[s][:, :],
                                                 INV[s], None, ALU.mult))
                    dve.sem_inc(acc_taken, 1)

                for n, v in enumerate((0.125, -0.125)):
                    chain.step(dve.memset(eighth[:, n:n + 1], v))
                row_max(0, 0)
                threshold(0, 0)
                row_max(1, 1)
                with dve.Fori(0, NT // 2 - 1) as i:
                    chain.loop(i, 2 * 20)
                    for s in range(2):
                        t = i * 2 + 1 + s
                        threshold(t, (1 + s) % 2)
                        scale(i * 2 + s, s)
                        row_max(i * 2 + 2 + s, s)
                chain.end(NT // 2 - 1)
                threshold(NT - 1, 1)
                scale(NT - 2, 0)
                scale(NT - 1, 1)



def gate(nc, name, w, terms, ones_row, bias_rows, mode, E=8):
    with Stage(nc, name) as st:
        bank = st.ps("bank", [P, NT, E])
        top = st.sb("top", [P, NT])
        tot = st.sb("tot", [P, NT])
        prob = st.sb("prob", [P, NT, E])
        rest = st.sb("rest", [P, NT, E])
        summed = st.sem("summed")
        logit_ready = st.sem("logit_ready")
        exp_ready = st.sem("exp_ready")
        step = st.sem("step")
        with nc.Block() as block:
            @block.tensor
            def _(pe):
                for t in range(NT):
                    rows = [(aT[:, t * P:(t + 1) * P], g) for aT, g in terms]
                    rows += [(ones_row, b) for b in bias_rows]
                    for n, (lhsT, rhs) in enumerate(rows):
                        last = pe.matmul(bank[:, t, :], lhsT, rhs, start=n == 0, stop=n == len(rows) - 1)
                last.then_inc(summed, 1)

            @block.vector
            def _(dve):
                chain = Chain(dve, step)
                dve.wait_ge(summed, 1)
                chain.step(dve.tensor_reduce(top[:, :], bank[:, :, :], axis=AX.X, op=ALU.max))
                dve.tensor_tensor(prob[:, :, :], bank[:, :, :], over(top[:, :], E),
                                  ALU.subtract).then_inc(logit_ready, 1)
                dve.wait_ge(exp_ready, 1)
                if mode != "softmax2":
                    chain.step(dve.tensor_reduce(tot[:, :], prob[:, :, :], axis=AX.X, op=ALU.add))
                    chain.step(dve.reciprocal(tot[:, :], tot[:, :]))
                    chain.step(dve.tensor_tensor(prob[:, :, :], prob[:, :, :], over(tot[:, :], E), ALU.mult))
                chain.step(dve.tensor_reduce(top[:, :], prob[:, :, :], axis=AX.X, op=ALU.max))
                if mode != "top1":
                    chain.step(dve.tensor_tensor(rest[:, :, :], prob[:, :, :], over(top[:, :], E), ALU.is_ge))
                    chain.step(dve.scalar_tensor_tensor(rest[:, :, :], rest[:, :, :], -4.0, prob[:, :, :],
                                                        ALU.mult, ALU.add))
                    chain.step(dve.tensor_reduce(top[:, :], rest[:, :, :], axis=AX.X, op=ALU.max))
                chain.step(dve.tensor_tensor(rest[:, :, :], prob[:, :, :], over(top[:, :], E), ALU.is_ge))
                chain.step(dve.tensor_tensor(w, prob[:, :, :], rest[:, :, :], ALU.mult))
                if mode != "top1":
                    chain.step(dve.tensor_reduce(tot[:, :], w, axis=AX.X, op=ALU.add))
                    if mode == "top2":
                        chain.step(dve.tensor_scalar(tot[:, :], tot[:, :], 1e-9, None, ALU.add))
                    chain.step(dve.reciprocal(tot[:, :], tot[:, :]))
                    chain.step(dve.tensor_tensor(w, w, over(tot[:, :], E), ALU.mult))

            @block.scalar
            def _(act):
                act.wait_ge(logit_ready, 1)
                act.activation(prob[:, :, :], prob[:, :, :], ACT.Exp).then_inc(exp_ready, 1)


def transpose_gates(nc, name, w, wT, ident, E=8):
    with Stage(nc, name) as st:
        banks = [st.ps(f"bank{k}", [E, CH]) for k in range(NCH)]
        turned = st.sem("turned")
        with nc.Block() as block:
            @block.tensor
            def _(pe):
                for k in range(NCH):
                    for j in range(TPC):
                        last = pe.transpose(banks[k][:, j * P:(j + 1) * P], w[:, k * TPC + j, :], ident)
                    last.then_inc(turned, 1)

            @block.scalar
            def _(act):
                for k in range(NCH):
                    act.wait_ge(turned, k + 1)
                    act.activation(wT[:, k * CH:(k + 1) * CH], banks[k][:, :], ACT.Copy)


def experts(nc, name, xT, wT, sel, win, wgate, bias, wout, bout, outT, sizes, func, E=8):
    hidden = sum(sizes)
    tiles = [(e, h, e * hidden + sum(sizes[:h]), n) for e in range(E) for h, n in enumerate(sizes)]
    M = len(tiles)
    with Stage(nc, name) as st:
        act_out = [st.sb(f"act_out{s}", [P, CH]) for s in range(2)]
        unit = [st.sb(f"unit{s}", [P, CH]) for s in range(2)]
        share = [st.sb(f"share{s}", [P, CH]) for s in range(2)]
        bc = st.ps("bc", [P, CH])
        up = [st.ps(f"up{s}", [P, CH]) for s in range(2)]
        gt = [st.ps(f"gt{s}", [P, CH]) for s in range(2)]
        acc = [st.ps(f"acc{s}", [P, CH]) for s in range(2)]
        share_ps = st.sem("share_ps")
        share_ready = st.sem("share_ready")
        share_used = st.sem("share_used")
        up_ready = st.sem("up_ready")
        act_ready = st.sem("act_ready")
        unit_ready = st.sem("unit_ready")
        unit_used = st.sem("unit_used")
        acc_ready = st.sem("acc_ready")
        acc_taken = st.sem("acc_taken")
        step = st.sem("step")
        with nc.Block() as block:
            @block.tensor
            def _(pe):
                pe.sem_inc(share_ready, 1)
                pe.sem_inc(acc_taken, 1)
                pe.sem_inc(unit_ready, 2)

                def down(i, n):
                    e, h, at, m = tiles[n]
                    pe.wait_ge(unit_ready, i * M + n + 3)
                    return pe.matmul(acc[0][:, :], wout[0:m, n * C:(n + 1) * C], unit[n % 2][0:m, :],
                                     start=n == 0, stop=bout is None and n == M - 1).then_inc(unit_used, 1)

                with pe.Fori(0, NCH) as i:
                    cols = bass.ds(i * CH, CH)
                    for n, (e, h, at, m) in enumerate(tiles):
                        if h == 0:
                            pe.wait_ge(share_ready, i * E + e + 1)
                        pe.wait_ge(unit_ready, i * M + n + 1)
                        last = pe.matmul(up[n % 2][0:m, :], win[:, at:at + m], xT[:, cols], start=True, stop=True)
                        if wgate is not None:
                            last = pe.matmul(gt[n % 2][0:m, :], wgate[:, at:at + m], xT[:, cols],
                                             start=True, stop=True)
                        last.then_inc(up_ready, 1)
                        if h == 0:
                            pe.matmul(bc[:, :], sel[0:E, e * P:(e + 1) * P], wT[:, cols],
                                      start=True, stop=True).then_inc(share_ps, 1)
                        if n == 1:
                            pe.wait_ge(acc_taken, i + 1)
                        if n:
                            down(i, n - 1)
                    last = down(i, M - 1)
                    if bout is not None:
                        pe.matmul(acc[0][:, :], bout, wT[:, cols], start=False, stop=True)
                    pe.drain().then_inc(acc_ready, 1)

            @block.scalar
            def _(act):
                with act.Fori(0, NCH) as i:
                    for n, (e, h, at, m) in enumerate(tiles):
                        if h == 0:
                            act.wait_ge(share_ps, i * E + e + 1)
                            act.wait_ge(share_used, i * E + e + 1)
                            act.activation(share[e % 2][:, :], bc[:, :], ACT.Copy).then_inc(share_ready, 1)
                        act.wait_ge(up_ready, i * M + n + 1)
                        act.wait_ge(unit_ready, i * M + n + 1)
                        act.activation(act_out[n % 2][0:m, :], up[n % 2][0:m, :], func,
                                       bias=bias[0:m, n:n + 1] if bias is not None else 0.0)\
                           .then_inc(act_ready, 1)
                    act.wait_ge(acc_ready, i + 1)
                    act.activation(outT[:, bass.ds(i * CH, CH)], acc[0][:, :], ACT.Copy).then_inc(acc_taken, 1)

            @block.vector
            def _(dve):
                chain = Chain(dve, step)
                dve.sem_inc(unit_used, 2)
                dve.sem_inc(share_used, 2)
                with dve.Fori(0, NCH) as i:
                    if wgate is not None:
                        chain.loop(i, M)
                    for n, (e, h, at, m) in enumerate(tiles):
                        dve.wait_ge(act_ready, i * M + n + 1)
                        src = act_out[n % 2][0:m, :]
                        if wgate is not None:
                            chain.step(dve.tensor_tensor(src, src, gt[n % 2][0:m, :], ALU.mult))
                        if h == 0:
                            dve.wait_ge(share_ready, i * E + e + 2)
                        dve.wait_ge(unit_used, i * M + n + 1)
                        last = dve.tensor_tensor(unit[n % 2][0:m, :], src, share[e % 2][0:m, :],
                                                 ALU.mult).then_inc(unit_ready, 1)
                        if h == len(sizes) - 1:
                            dve.wait_ge(unit_ready, i * M + n + 3)
                            dve.sem_inc(share_used, 1)
                if wgate is not None:
                    chain.end(NCH)



def rope(nc, name, outs, xT, w, w_rot, cos_d, sin_d):
    m = outs.shape[0]
    with Stage(nc, name) as st:
        cos = st.sb("cos", [m, N])
        sin = st.sb("sin", [m, N])
        tmp = [st.sb(f"tmp{b}", [m, CH]) for b in range(2)]
        a = [st.ps(f"a{b}", [m, CH]) for b in range(2)]
        r = [st.ps(f"r{b}", [m, CH]) for b in range(2)]
        loaded = st.sem("loaded")
        ready = st.sem("ready")
        step = st.sem("step")
        with nc.Block() as block:
            @block.sync
            def _(sp):
                sp.dma_start(cos[:, :], cos_d[0:m, :]).then_inc(loaded, 16)
                sp.dma_start(sin[:, :], sin_d[0:m, :]).then_inc(loaded, 16)

            @block.tensor
            def _(pe):
                for k in range(NCH):
                    if k >= 2:
                        pe.wait_ge(step, 3 * (k - 1))
                    pe.matmul(a[k % 2][:, :], w, xT[:, k * CH:(k + 1) * CH], start=True, stop=True)
                    pe.matmul(r[k % 2][:, :], w_rot, xT[:, k * CH:(k + 1) * CH], start=True,
                              stop=True).then_inc(ready, 1)

            @block.vector
            def _(dve):
                chain = Chain(dve, step)
                dve.wait_ge(loaded, 32)
                for k in range(NCH):
                    s = slice(k * CH, (k + 1) * CH)
                    dve.wait_ge(ready, k + 1)
                    chain.step(dve.tensor_tensor(outs[:, s], a[k % 2][:, :], cos[:, s], ALU.mult))
                    chain.step(dve.tensor_tensor(tmp[k % 2][:, :], r[k % 2][:, :], sin[:, s], ALU.mult))
                    chain.step(dve.tensor_tensor(outs[:, s], outs[:, s], tmp[k % 2][:, :], ALU.add))


def causal_attention(nc, name, q_d, kT, v, y, mask, ident, scale):
    HD = 32
    KV = 2
    GT = TPC * 2
    groups = [(g, kv) for g in range(NCH) for kv in range(KV)]
    with Stage(nc, name) as st:
        q = [st.sb(f"q{s}", [HD, P]) for s in range(2)]
        score = [st.sb(f"score{s}", [P, N]) for s in range(2)]
        probT = st.sb("probT", [P, N])
        small = st.sb("small", [P, 2, 4])
        NEG, SUM, INV, MAX = ([small[:, s, n:n + 1] for s in range(2)] for n in range(4))
        sc = [st.ps(f"sc{b}", [P, CH]) for b in range(2)]
        own = [st.ps(f"own{b}", [P, CH]) for b in range(2)]
        tr = [st.ps(f"tr{b}", [P, CH]) for b in range(2)]
        acc = [st.ps(f"acc{s}", [P, HD]) for s in range(2)]
        q_ready = [st.sem(f"q_ready{s}") for s in range(2)]
        sc_ready = st.sem("sc_ready")
        sc_copied = st.sem("sc_copied")
        own_ready = st.sem("own_ready")
        own_masked = st.sem("own_masked")
        neg_ready = st.sem("neg_ready")
        exp_ready = st.sem("exp_ready")
        turned = st.sem("turned")
        turned_taken = st.sem("turned_taken")
        acc_ready = st.sem("acc_ready")
        step = st.sem("step")

        max_ready = st.sem("max_ready")
        inv_ready = st.sem("inv_ready")

        def tile(n, j, s):
            return j * 2 + (n * GT + s)

        def earlier(n, j, s):
            g = n // KV
            return j * (2 * g) + (KV * GT * g * (g - 1) // 2 + (n % KV) * GT * g + s * g)

        def blocks(n, j, s):
            w = n // KV + 1
            return j * (2 * w) + (KV * GT * w * (w - 1) // 2 + (n % KV) * GT * w + s * w)

        def tiles(eng, first, each):
            first(0, 0, 0)
            for n in range(len(groups)):
                with eng.Fori(0, TPC - 1) as i:
                    first(n, i, 1)
                    each(n, i, 0)
                    first(n, i + 1, 0)
                    each(n, i, 1)
                first(n, TPC - 1, 1)
                each(n, TPC - 1, 0)
                if n + 1 < len(groups):
                    first(n + 1, 0, 0)
                each(n, TPC - 1, 1)

        with nc.Block() as block:
            @block.sync
            def _(sp):
                for t in range(2):
                    sp.dma_start(q[t][:, :], q_d[:, t, :]).then_inc(q_ready[t], 16)
                with sp.Fori(1, len(groups) * GT // 2) as i:
                    for s in range(2):
                        sp.wait_ge(own_ready, i * 2 + (s - 1))
                        sp.dma_start(q[s][:, :], q_d[:, bass.ds(i * 2 + s, 1), :]
                                     .rearrange("p o c -> p (o c)")).then_inc(q_ready[s], 16)

            @block.tensor
            def _(pe):
                def scores(n, j, s):
                    g, kv = groups[n]
                    pe.wait_ge(q_ready[s], j * 16 + (n * GT // 2 * 16 + 16))
                    for c in range(g):
                        pe.wait_ge(sc_copied, earlier(n, j, s) + (c + 1))
                        pe.matmul(sc[(s * g + c) % 2][:, :], q[s][:, :],
                                  kT[:, kv * N + c * CH:kv * N + (c + 1) * CH], start=True,
                                  stop=True).then_inc(sc_ready, 1)
                    pe.wait_ge(own_masked, tile(n, j, s) + 1)
                    pe.matmul(own[s][:, :], q[s][:, :], kT[:, kv * N + g * CH:kv * N + (g + 1) * CH],
                              start=True, stop=True).then_inc(own_ready, 1)

                def transpose4(n, j, s, k):
                    w = groups[n][0] + 1
                    pe.wait_ge(turned_taken, blocks(n, j, s) + (k + 1))
                    for b in range(TPC):
                        at = (k * TPC + b) * P
                        last = pe.transpose(tr[(s * w + k) % 2][:, b * P:(b + 1) * P],
                                            score[s][:, at:at + P], ident)
                    last.then_inc(turned, 1)

                def weigh(n, j, s):
                    g, kv = groups[n]
                    w = g + 1
                    pe.wait_ge(exp_ready, tile(n, j, s) + 1)
                    for k in range(min(w, 2)):
                        transpose4(n, j, s, k)
                    for k in range(w):
                        pe.wait_ge(turned_taken, blocks(n, j, s) + (k + 3))
                        for b in range(k * TPC, (k + 1) * TPC):
                            last = pe.matmul(acc[s][:, :], probT[:, b * P:(b + 1) * P], v[:, kv, b, :],
                                             start=b == 0, stop=b == w * TPC - 1)
                        if k + 2 < w:
                            transpose4(n, j, s, k + 2)
                    last.then_inc(acc_ready, 1)

                pe.sem_inc(sc_copied, 2)
                pe.sem_inc(own_masked, 2)
                pe.sem_inc(turned_taken, 2)
                tiles(pe, scores, weigh)

            @block.scalar
            def _(act):
                def softmax(n, j, s):
                    g, kv = groups[n]
                    for c in range(g):
                        act.wait_ge(sc_ready, earlier(n, j, s) + (c + 1))
                        act.activation(score[s][:, c * CH:(c + 1) * CH], sc[(s * g + c) % 2][:, :],
                                       ACT.Copy).then_inc(sc_copied, 1)
                    act.wait_ge(neg_ready, tile(n, j, s) + 1)
                    act.activation(score[s][:, 0:(g + 1) * CH], score[s][:, 0:(g + 1) * CH], ACT.Exp,
                                   bias=NEG[s], scale=scale, accum_out=SUM[s]).then_inc(exp_ready, 1)

                tiles(act, softmax, lambda n, j, s: None)

            @block.vector
            def _(dve):
                def row_max(n, j, s):
                    g, kv = groups[n]
                    dve.wait_ge(own_ready, tile(n, j, s) + 1)
                    dve.tensor_tensor(score[s][:, g * CH:(g + 1) * CH], own[s][:, :],
                                      mask[:, bass.ds(j * CH, CH)], ALU.add).then_inc(own_masked, 1)
                    dve.wait_ge(own_masked, tile(n, j, s) + 3)
                    if g:
                        dve.wait_ge(sc_copied, earlier(n, j, s) + (g + 2))
                    dve.tensor_reduce(MAX[s], score[s][:, 0:(g + 1) * CH], axis=AX.X,
                                      op=ALU.max).then_inc(max_ready, 1)
                    dve.wait_ge(max_ready, tile(n, j, s) + 1)
                    dve.tensor_scalar(NEG[s], MAX[s], -scale, None, ALU.mult).then_inc(neg_ready, 1)

                def take(n, j, s):
                    g, kv = groups[n]
                    w = g + 1
                    for k in range(w):
                        dve.wait_ge(turned, blocks(n, j, s) + (k + 1))
                        dve.tensor_copy(probT[:, k * CH:(k + 1) * CH],
                                        tr[(s * w + k) % 2][:, :]).then_inc(turned_taken, 1)
                    dve.wait_ge(exp_ready, tile(n, j, s) + 1)
                    dve.reciprocal(INV[s], SUM[s]).then_inc(inv_ready, 1)
                    dve.wait_ge(inv_ready, tile(n, j, s) + 1)
                    dve.wait_ge(acc_ready, tile(n, j, s) + 1)
                    dve.tensor_scalar(flat(y)[:, bass.ds(j * C + (g * TPC * C + kv * 2 * HD + s * HD), HD)],
                                      acc[s][:, :], INV[s], None, ALU.mult)

                tiles(dve, row_max, take)



def conv_silu(nc, name, a, u, w, bias):
    K = 4
    with Stage(nc, name) as st:
        step = st.sem("step")
        with nc.Block() as block:
            @block.vector
            def _(dve):
                chain = Chain(dve, step)
                chain.step(dve.tensor_scalar(u, a, w[:, K - 1:K], None, ALU.mult))
                for back in range(1, K):
                    chain.step(dve.scalar_tensor_tensor(u[:, back:], a[:, :N - back], w[:, K - 1 - back:K - back],
                                                        u[:, back:], ALU.mult, ALU.add))

            @block.scalar
            def _(act):
                act.wait_ge(step, K)
                act.activation(u, u, ACT.Silu, bias=bias)


ATANH = np.polynomial.chebyshev.Chebyshev.interpolate(
    lambda q: 2 * np.arctanh(np.sqrt(q)) / np.sqrt(q), 5, domain=[0, 1 / 9]
).convert(kind=np.polynomial.Polynomial).coef


def softplus(nc, name, dt, e, s, q):
    with Stage(nc, name) as st:
        step = st.sem("step")
        mag = st.sem("mag")
        squared = st.sem("squared")
        with nc.Block() as block:
            @block.scalar
            def _(act):
                act.activation(e, dt, ACT.Abs).then_inc(mag, 1)
                act.wait_ge(mag, 1)
                act.activation(e, e, ACT.Exp, scale=-1.0).then_inc(mag, 1)
                act.wait_ge(step, 3)
                act.activation(q, s, ACT.Square).then_inc(squared, 1)

            @block.vector
            def _(dve):
                chain = Chain(dve, step)
                dve.wait_ge(mag, 2)
                chain.step(dve.tensor_scalar(s, e, 2.0, None, ALU.add))
                chain.step(dve.reciprocal(s, s))
                chain.step(dve.tensor_tensor(s, s, e, ALU.mult))
                dve.wait_ge(squared, 1)
                chain.step(dve.tensor_scalar(e, q, float(ATANH[-1]), None, ALU.mult))
                for c in ATANH[-2:0:-1]:
                    chain.step(dve.scalar_tensor_tensor(e, e, float(c), q, ALU.add, ALU.mult))
                chain.step(dve.scalar_tensor_tensor(e, e, float(ATANH[0]), s, ALU.add, ALU.mult))
                chain.step(dve.scalar_tensor_tensor(dt, dt, 0.0, e, ALU.max, ALU.add))


def scan(nc, name, ys, dt, u, bT, cT, A, sel, ident):
    S = 16
    D = 2
    LC = 1024
    HC = LC // CH
    with Stage(nc, name) as st:
        bb = [st.sb(f"bb{s}", [P, LC]) for s in range(2)]
        cb = [st.sb(f"cb{s}", [P, LC]) for s in range(2)]
        dA = [st.sb(f"dA{s}", [P, LC]) for s in range(2)]
        h = [st.sb(f"h{s}", [P, LC]) for s in range(2)]
        dtu = [[st.sb(f"dtu{s}{d}", [P, LC]) for d in range(D)] for s in range(2)]
        dbu = st.sb("dbu", [P, LC])
        hc = [st.sb(f"hc{s}", [P, LC]) for s in range(2)]
        state = st.sb("state", [P, S * D])
        b_ps = st.ps("b_ps", [P, LC])
        c_ps = st.ps("c_ps", [P, LC])
        y_ps = [st.ps(f"y_ps{d}", [P, LC]) for d in range(D)]
        bc_ready = st.sem("bc_ready")
        bc_copied = st.sem("bc_copied")
        bc_used = st.sem("bc_used")
        dA_ready = st.sem("dA_ready")
        h_ready = st.sem("h_ready")
        hc_ready = st.sem("hc_ready")
        hc_used = st.sem("hc_used")
        dbu_ready = st.sem("dbu_ready")
        saved = st.sem("saved")
        y_ready = st.sem("y_ready")
        y_taken = st.sem("y_taken")
        dtu_ready = st.sem("dtu_ready")
        passed = st.sem("passed")
        with nc.Block() as block:
            @block.gpsimd
            def _(pool):
                with pool.Fori(0, N // LC // 2) as i:
                    for s in range(2):
                        pool.wait_ge(h_ready, i * (2 * S * D) + (s * S * D + 1))
                        for d in range(D):
                            at = bass.ds(i * (2 * LC) + s * LC, LC)
                            pool.tensor_tensor(dtu[s][d][:, :], dt[d][:, at], u[d][:, at],
                                               ALU.mult).then_inc(dtu_ready, 1)

            @block.tensor
            def _(pe):
                pe.sem_inc(bc_copied, 1)
                pe.sem_inc(y_taken, 1)

                def add(i, n, d):
                    m = n * D + d
                    pe.wait_ge(hc_ready, i * (S * D) + m + 1)
                    for c in range(HC):
                        last = pe.matmul(y_ps[d][:, c * CH:(c + 1) * CH], ident,
                                         hc[m % 2][:, c * CH:(c + 1) * CH], start=n == 0, stop=n == S - 1)
                    last.then_inc(hc_used, 1)

                def spread(i, n):
                    pe.wait_ge(bc_copied, i * S + n + 1)
                    pe.sem_inc(passed, 1)
                    for of, to in ((bT, b_ps), (cT, c_ps)):
                        for c in range(HC):
                            last = pe.matmul(to[:, c * CH:(c + 1) * CH], sel[:, n * P:(n + 1) * P],
                                             of[:, bass.ds(i * LC + c * CH, CH)], start=True, stop=True)
                    last.then_inc(bc_ready, 1)

                with pe.Fori(0, N // LC) as i:
                    spread(i, 0)
                    pe.wait_ge(y_taken, i + 1)
                    for n in range(S):
                        if n + 1 < S:
                            spread(i, n + 1)
                        for d in range(D):
                            add(i, n, d)
                    pe.drain().then_inc(y_ready, 1)

            @block.scalar
            def _(act):
                def decay(i, n, d):
                    m = n * D + d
                    act.wait_ge(h_ready, i * (S * D) + m + 1)
                    act.sem_inc(passed, 1)
                    act.activation(dA[m % 2][:, :], dt[d][:, bass.ds(i * LC, LC)], ACT.Exp,
                                   scale=A[:, d * S + n:d * S + n + 1]).then_inc(dA_ready, 1)

                with act.Fori(0, N // LC) as i:
                    for n in range(S):
                        act.wait_ge(bc_ready, i * S + n + 1)
                        act.wait_ge(bc_used, i * S + n + 1)
                        act.activation(bb[n % 2][:, :], b_ps[:, :], ACT.Copy)
                        act.activation(cb[n % 2][:, :], c_ps[:, :], ACT.Copy).then_inc(bc_copied, 1)
                        for d in range(D):
                            decay(i, n, d)
                    act.wait_ge(y_ready, i + 1)
                    act.sem_inc(passed, 1)
                    for d in range(D):
                        last = act.activation(ys[d][:, bass.ds(i * LC, LC)], y_ps[d][:, :], ACT.Copy)
                    last.then_inc(y_taken, 1)

            @block.vector
            def _(dve):
                dve.memset(state[:, :], 0.0).then_inc(saved, 1)
                dve.sem_inc(h_ready, 2)
                dve.sem_inc(hc_used, 2)
                dve.sem_inc(bc_used, 2)
                with dve.Fori(0, N // LC // 2) as turn:
                    for s in range(2):
                        i = turn * 2 + s
                        dve.wait_ge(dtu_ready, i * D + D)
                        for n in range(S):
                            dve.wait_ge(bc_copied, i * S + n + 2)
                            for d in range(D):
                                m = n * D + d
                                at = i * (S * D) + m
                                dve.tensor_tensor(dbu[:, :], dtu[s][d][:, :], bb[n % 2][:, :],
                                                  ALU.mult).then_inc(dbu_ready, 1)
                                dve.wait_ge(dbu_ready, at + 1)
                                dve.wait_ge(dA_ready, at + 1)
                                dve.wait_ge(saved, at + 1)
                                dve.tensor_tensor_scan(h[m % 2][:, :], dA[m % 2][:, :], dbu[:, :],
                                                       state[:, m:m + 1], ALU.mult, ALU.add).then_inc(h_ready, 1)
                                dve.wait_ge(h_ready, at + 3)
                                dve.tensor_copy(state[:, m:m + 1], h[m % 2][:, LC - 1:LC]).then_inc(saved, 1)
                                dve.wait_ge(hc_used, at + 1)
                                dve.tensor_tensor(hc[m % 2][:, :], h[m % 2][:, :], cb[n % 2][:, :],
                                                  ALU.mult).then_inc(hc_ready, 1)
                            dve.wait_ge(hc_ready, i * (S * D) + (n + 1) * D)
                            dve.sem_inc(bc_used, 1)



def routed_add(nc, name, x, hT, w, wd, bd, ones_row, hid_tiles, E=8):
    HALF = E * C // 2
    with Stage(nc, name) as st:
        ht = [st.sb(f"ht{s}", [P, hid_tiles, P]) for s in range(2)]
        part = [st.sb(f"part{s}", [P, E, C]) for s in range(2)]
        total = [st.sb(f"total{s}", [P, C]) for s in range(2)]
        bank = [[st.ps(f"bank{s}{h}", [P, HALF]) for h in range(2)] for s in range(2)]
        ht_ready = st.sem("ht_ready")
        y_ready = st.sem("y_ready")
        y_taken = st.sem("y_taken")
        sum_step = st.sem("sum_step")
        xf = flat(x)
        wf = flat(w)
        with nc.Block() as block:
            @block.gpsimd
            def _(pool):
                for s in range(2):
                    pool.tensor_copy(ht[s][:, :, :], hT[:, :, s * P:(s + 1) * P]).then_inc(ht_ready, 1)
                with pool.Fori(1, NT // 2) as i:
                    for s in range(2):
                        pool.wait_ge(y_ready, i * 4 + (s - 1) * 2)
                        pool.tensor_copy(ht[s][:, :, :],
                                         hT[:, :, bass.ds(i * (2 * P) + s * P, P)]).then_inc(ht_ready, 1)

            @block.tensor
            def _(pe):
                pe.sem_inc(y_taken, 4)
                with pe.Fori(0, NT // 2) as i:
                    for s in range(2):
                        pe.wait_ge(ht_ready, i * 2 + (s + 1))
                        for h in range(2):
                            pe.wait_ge(y_taken, i * 4 + (s * 2 + h + 1))
                            for k in range(hid_tiles):
                                pe.matmul(bank[s][h][:, :], ht[s][:, k, :], wd[:, k, h * HALF:(h + 1) * HALF],
                                          start=k == 0, stop=False)
                            pe.matmul(bank[s][h][:, :], ones_row, bd[:, h * HALF:(h + 1) * HALF],
                                      start=False, stop=True).then_inc(y_ready, 1)

            @block.vector
            def _(dve):
                chain = Chain(dve, sum_step)
                with dve.Fori(0, NT // 2) as i:
                    chain.loop(i, 4)
                    for s in range(2):
                        for h in range(2):
                            dve.wait_ge(y_ready, i * 4 + (s * 2 + h + 1))
                            g = wf[:, bass.ds(i * (2 * E) + (s * E + h * (E // 2)), E // 2)]
                            dve.tensor_tensor(part[s][:, h * (E // 2):(h + 1) * (E // 2), :],
                                              bank[s][h][:, :].rearrange("p (e c) -> p e c", c=C),
                                              over(g, C), ALU.mult).then_inc(y_taken, 1)
                        dve.wait_ge(y_taken, i * 4 + (s * 2 + 2 + 4))
                        chain.step(dve.tensor_reduce(total[s][:, :], part[s][:, :, :].rearrange("p e c -> p c e"),
                                                     axis=AX.X, op=ALU.add))
                        at = bass.ds(i * (2 * C) + s * C, C)
                        chain.step(dve.tensor_tensor(xf[:, at], xf[:, at], total[s][:, :], ALU.add))
                chain.end(NT // 2)



def vector_steps(nc, name, steps):
    with Stage(nc, name) as st:
        step = st.sem("step")
        with nc.Block() as block:
            @block.vector
            def _(dve):
                steps(dve, Chain(dve, step))


def block0(nc, d, x, ident, ones_row):
    with Stage(nc, "b0") as st:
        h = x
        xa = [st.sb(f"xa{n}", [P, NT, C]) for n in range(2)]
        rinv = st.sb("rinv", [P, NT])
        u1 = st.sb("u1", [P, 2 * C])
        u2 = st.sb("u2", [P, 2 * C])
        w1, w2, w3 = st.sb("w1", [P, 64]), st.sb("w2", [64, 64]), st.sb("w3", [P, 64])
        load(nc, "b0load", [(u1[:, :], d["L0_U1"]), (u2[:, :], d["L0_U2"]), (w1[:, :], d["L0_W1"]),
                            (w2[:, :], d["L0_W2"]), (w3[:, :], d["L0_W3"])])
        vector_steps(nc, "b0r", lambda dve, chain: (
            chain.step(dve.tensor_scalar(rinv[:, :], d["rowsum"][:, :], 1.0, None, ALU.add)),
            chain.step(dve.reciprocal(rinv[:, :], rinv[:, :]))))
        norm(nc, "b0n", x, xa[0], None, ident, 1e-5)
        vector_steps(nc, "b0c", lambda dve, chain: (
            chain.step(dve.tensor_copy(h[:, :, :], xa[0][:, :, :])),))
        with Stage(nc, "b0f") as s2:
            fT = s2.sb("fT", [P, N])
            xf = s2.sb("xf", [P, NT, C])
            vector_steps(nc, "b0d", lambda dve, chain: chain.step(
                dve.tensor_copy(xf[:, :, :], xa[0][:, :, :])))
            for n in range(2):
                aggregate(nc, f"b0g1{n}", d["adj_t"], xf, fT)

                def normed(dve, chain, k, bank):
                    s = slice(k * TPC, (k + 1) * TPC)
                    chain.step(dve.tensor_tensor(xf[:, s, :], bank, xf[:, s, :], ALU.add))
                    chain.step(dve.tensor_tensor(xf[:, s, :], xf[:, s, :], over(rinv[:, s], C), ALU.mult))
                to_nodes(nc, f"b0g2{n}", fT, ident, normed)
                to_channels(nc, f"b0g3{n}", xf, fT, ident)
                project_add(nc, f"b0u1{n}", h, [(fT, u1[:, n * C:(n + 1) * C])], ones_row)
        for n in range(2):
            a, b = xa[n], xa[1 - n]
            with Stage(nc, f"b0q{n}") as s2:
                qT, kT = s2.sb("qT", [64, N]), s2.sb("kT", [64, N])
                with Stage(nc, f"b0p{n}") as s3:
                    aT, q1T = s3.sb("aT", [P, N]), s3.sb("q1T", [64, N])
                    to_channels(nc, f"b0t{n}", a, aT, ident)
                    project_T(nc, f"b0q1{n}", q1T, [(w1[:, :], aT)])
                    project_T(nc, f"b0q2{n}", qT, [(w2[:, :], q1T)])
                    project_T(nc, f"b0k{n}", kT, [(w3[:, :], aT)])
                top_p_attention(nc, f"b0a{n}", qT, kT, a, b, ident)
            with Stage(nc, f"b0v{n}") as s2:
                bT = s2.sb("bT", [P, N])
                to_channels(nc, f"b0g4{n}", b, bT, ident)
                project_add(nc, f"b0u2{n}", h, [(bT, u2[:, n * C:(n + 1) * C])], ones_row)
        gb = st.sb("gb", [P, 2, C])
        xf = xa[0]
        norm(nc, "b0m", h, xf, None, ident, 1e-5)
        load(nc, "b0gb", [(gb[:, 0, :], d["L0_g"]), (gb[:, 1, :], d["L0_b"]), (flat(x[:, :, :]), d["x"])])

        def affine(dve, chain):
            g, b = (gb[:, n:n + 1, :].to_broadcast([P, NT, C]) for n in range(2))
            chain.step(dve.tensor_tensor(xf[:, :, :], xf[:, :, :], g, ALU.mult))
            chain.step(dve.tensor_tensor(x[:, :, :], x[:, :, :], b, ALU.add))
            chain.step(dve.tensor_tensor(x[:, :, :], x[:, :, :], xf[:, :, :], ALU.add))
        vector_steps(nc, "b0z", affine)
    with Stage(nc, "f0") as st:
        xn, xT = st.sb("xn", [P, NT, C]), st.sb("xT", [P, N])
        w, b = st.sb("w", [P, C]), st.sb("b", [1, C])
        load(nc, "f0l", [(w[:, :], d["L0f_w"]), (b[:, :], d["L0f_b"])])
        norm(nc, "f0n", x, xn, xT, ident, 1e-5)
        project_add(nc, "f0p", x, [(xT, w[:, :])], ones_row, b[:, :])


def block1_graph(nc, d, x, ident, ones_row):
    with Stage(nc, "g1") as st:
        xn, xT, aT = st.sb("xn", [P, NT, C]), st.sb("xT", [P, N]), st.sb("aT", [P, N])
        w, wc, b = st.sb("w", [P, 2 * C]), st.sb("wc", [P, C]), st.sb("b", [1, C])
        load(nc, "g1l", [(w[:, :], d["L1g_w"]), (wc[:, :], d["L1g_wc"]), (b[:, :], d["L1g_b"])])
        norm(nc, "g1n", x, xn, xT, ident, 1e-5)
        aggregate(nc, "g1a", d["adj_t"], xn, aT)

        def edges(dve, chain, s):
            e = over(d["edge"][:, s], C)
            chain.step(dve.tensor_tensor(xn[:, s, :], wc[:, :].unsqueeze(1).to_broadcast([P, TPC, C]), e, ALU.mult))
            chain.step(dve.tensor_tensor(x[:, s, :], x[:, s, :], xn[:, s, :], ALU.add))
        project_add(nc, "g1p", x, [(xT, w[:, 0:C]), (aT, w[:, C:2 * C])], ones_row, b[:, :], edges)


def block1_ffn(nc, d, x, ident, ones_row, sel):
    HD, KV = 32, 2
    with Stage(nc, "f1") as st:
        xl = st.sb("xl", [P, NT, C])
        cols = st.sb("cols", [P, 2])
        load(nc, "f1c", [(cols[:, :], d["L1f_ln"])])
        norm(nc, "f1n", x, xl, None, ident, 1e-5)
        vector_steps(nc, "f1y", lambda dve, chain: chain.step(
            dve.tensor_tensor(x[:, :, :], x[:, :, :], xl[:, :, :], ALU.add)))
        with Stage(nc, "f1a") as s1:
            y = s1.sb("y", [P, NT, C])
            with Stage(nc, "f1b") as s2:
                kT = s2.sb("kT", [HD, KV * N])
                v = s2.sb("v", [P, KV, NT, HD])
                with Stage(nc, "f1c") as s3:
                    hT = s3.sb("hT", [P, N])
                    qr = s3.sb("qr", [P, N])
                    kr = s3.sb("kr", [KV * HD, N])
                    wq, wk, wv = s3.sb("wq", [P, 2 * C]), s3.sb("wk", [P, 2 * 64]), s3.sb("wv", [P, 64])
                    load(nc, "f1w", [(wq[:, :], d["L1f_wq"]), (wk[:, :], d["L1f_wk"]), (wv[:, :], d["L1f_wv"])])
                    norm(nc, "f1m", xl, y, hT, ident, 1e-6, center=False, gamma=cols[:, 0:1])
                    rope(nc, "f1q", qr, hT, wq[:, 0:C], wq[:, C:2 * C], d["cos"], d["sin"])
                    rope(nc, "f1k", kr, hT, wk[:, 0:64], wk[:, 64:128], d["cos"], d["sin"])
                    values(nc, "f1V", v, hT, wv)
                    with Stage(nc, "f1d") as s4:
                        stored = s4.sem("stored")
                        with nc.Block() as block:
                            @block.sync
                            def _(sp):
                                for hd in range(4):
                                    kv, s = hd // 2, hd % 2
                                    for g in range(NCH):
                                        sp.dma_start(d["q_dram"][:, g, kv, :, s, :],
                                                     qr[hd * HD:(hd + 1) * HD, g * CH:(g + 1) * CH]
                                                     .rearrange("p (j c) -> p j c", c=P)).then_inc(stored, 16)
                                for kv in range(KV):
                                    sp.dma_start(kT[:, kv * N:(kv + 1) * N],
                                                 kr[kv * HD:(kv + 1) * HD, :]).then_inc(stored, 16)
                                sp.wait_ge(stored, 16 * (4 * NCH + KV))
                mask = s2.sb("mask", [P, TPC * CH])
                load(nc, "f1o", [(mask[:, :], d["mask"])])
                causal_attention(nc, "f1e", d["q_dram"].rearrange("p g k j s c -> p (g k j s) c"), kT, v, y[:, :, :], mask, ident, float(1.0 / np.sqrt(HD)))
            with Stage(nc, "f1f") as s2:
                yT, wo = s2.sb("yT", [P, N]), s2.sb("wo", [P, C])
                load(nc, "f1g", [(wo[:, :], d["L1f_wo"])])
                to_channels(nc, "f1h", y, yT, ident)
                project_add(nc, "f1i", xl, [(yT, wo[:, :])], ones_row)
                project_add(nc, "f1j", x, [(yT, wo[:, :])], ones_row)
        with Stage(nc, "f1r") as s1:
            fT, outT = s1.sb("fT", [P, N]), s1.sb("outT", [P, N])
            w, wT = s1.sb("w", [P, NT, 8]), s1.sb("wT", [8, N])
            wr = s1.sb("wr", [P, 8])
            w1, w3, w2 = s1.sb("w1", [P, 8 * 341]), s1.sb("w3", [P, 8 * 341]), s1.sb("w2", [P, 24 * C])
            load(nc, "f1s", [(wr[:, :], d["L1f_wr"]), (w1[:, :], d["L1f_w1"]), (w3[:, :], d["L1f_w3"]),
                             (w2[:, :], d["L1f_w2"])])
            norm(nc, "f1t", xl, xl, fT, ident, 1e-6, center=False, gamma=cols[:, 1:2])
            gate(nc, "f1u", w[:, :, :], [(fT, wr[:, :])], ones_row, [], "top2")
            transpose_gates(nc, "f1v", w, wT, ident)
            experts(nc, "f1w", fT, wT, sel, w1, w3, None, w2, None, outT, (128, 128, 85), ACT.Silu)
            add_T(nc, "f1x", x, outT, ident)


def add_T(nc, name, x, aT, ident):
    def add(dve, chain, k, bank):
        s = slice(k * TPC, (k + 1) * TPC)
        chain.step(dve.tensor_tensor(x[:, s, :], x[:, s, :], bank, ALU.add))
    to_nodes(nc, name, aT, ident, add)


def values(nc, name, v, hT, wv):
    with Stage(nc, name) as st:
        banks = [st.ps(f"bank{k}", [P, 8, 64]) for k in range(4)]
        ready = st.sem("ready")
        with nc.Block() as block:
            @block.tensor
            def _(pe):
                for t in range(NT):
                    last = pe.matmul(banks[t // 8][:, t % 8, :], hT[:, t * P:(t + 1) * P], wv[:, :],
                                     start=True, stop=True)
                    if t % 8 == 7:
                        last.then_inc(ready, 1)

            @block.vector
            def _(dve):
                for k in range(4):
                    dve.wait_ge(ready, k + 1)
                    dve.tensor_copy(v[:, :, k * 8:(k + 1) * 8, :],
                                    banks[k][:, :, :].rearrange("p t (h e) -> p h t e", e=32))


def block2_graph(nc, d, x, ident, ones_row, sel):
    with Stage(nc, "g2") as st:
        hT = st.sb("hT", [P, N])
        u = [st.sb(f"u{h}", [P, N]) for h in range(2)]
        names = dict(gcn=C, cols=3, w_in=512, conv=8, conv_b=2, w_xp=80, b_dt=2, A=32, D=2, w_out=2 * C)
        w = {n: st.sb(n, [P, m]) for n, m in names.items()}
        w_dt = st.sb("w_dt", [8, 256])
        load(nc, "g2l", [(w[n][:, :], d["L2g_" + n]) for n in names] + [(w_dt[:, :], d["L2g_w_dt"])])
        with Stage(nc, "g2a") as s1:
            xn, aT = s1.sb("xn", [P, NT, C]), s1.sb("aT", [P, N])
            norm(nc, "g2n", x, xn, None, ident, 1e-5)
            aggregate(nc, "g2g", d["adj_t"], xn, aT)
            project_T(nc, "g2p", hT, [(w["gcn"][:, :], aT)], ACT.Relu, w["cols"][:, 0:1])
            to_nodes(nc, "g2o", hT, ident, lambda dve, chain, k, bank: chain.step(
                dve.tensor_copy(xn[:, k * TPC:(k + 1) * TPC, :], bank)))
            norm(nc, "g2m", xn, xn, hT, ident, 1e-5, gamma=w["cols"][:, 1:2], beta=w["cols"][:, 2:3])
            for h in range(2):
                project_T(nc, f"g2x{h}", aT, [(w["w_in"][:, h * P:(h + 1) * P], hT)])
                conv_silu(nc, f"g2c{h}", aT[:, :], u[h][:, :], w["conv"][:, 4 * h:4 * h + 4], w["conv_b"][:, h:h + 1])
        with Stage(nc, "g2b") as s1:
            dt = [s1.sb(f"dt{h}", [P, N]) for h in range(2)]
            bT, cT = s1.sb("bT", [16, N]), s1.sb("cT", [16, N])
            tmp_stage = Stage(nc, "g2t")
            tmp = [tmp_stage.sb(f"tmp{h}", [P, N]) for h in range(3)]
            rank = tmp[0][0:8, :]
            for out, at, m in ((rank, 0, 8), (bT[:, :], 8, 16), (cT[:, :], 24, 16)):
                project_T(nc, f"g2d{at}", out, [(w["w_xp"][:, h * 40 + at:h * 40 + at + m], u[h]) for h in range(2)])
            for h in range(2):
                project_T(nc, f"g2e{h}", dt[h], [(w_dt[:, h * P:(h + 1) * P], rank)], bias=w["b_dt"][:, h:h + 1])
            for h in range(2):
                softplus(nc, f"g2f{h}", dt[h][:, :], *(t[:, :] for t in tmp))
            tmp_stage.__exit__(None)
            with Stage(nc, "g2i") as s2:
                e = s2.sem("e")
                with nc.Block() as block:
                    @block.scalar
                    def _(act):
                        act.activation(w["A"][:, :], w["A"][:, :], ACT.Exp).then_inc(e, 1)

                    @block.vector
                    def _(dve):
                        dve.wait_ge(e, 1)
                        dve.tensor_scalar(w["A"][:, :], w["A"][:, :], -1.0, None, ALU.mult)
            scan(nc, "g2s", dt, dt, u, bT, cT, w["A"], sel, ident)

            z = [s1.sb(f"z{h}", [P, N]) for h in range(2)]
            for h in range(2):
                project_T(nc, f"g2z{h}", z[h], [(w["w_in"][:, (2 + h) * P:(3 + h) * P], hT)], ACT.Silu)

            def out(dve, chain):
                for h in range(2):
                    chain.step(dve.scalar_tensor_tensor(dt[h][:, :], u[h][:, :], w["D"][:, h:h + 1], dt[h][:, :],
                                                        ALU.mult, ALU.add))
                    chain.step(dve.tensor_tensor(dt[h][:, :], dt[h][:, :], z[h][:, :], ALU.mult))
            vector_steps(nc, "g2y", out)
            project_add(nc, "g2w", x, [(dt[h], w["w_out"][:, h * C:(h + 1) * C]) for h in range(2)], ones_row)


def block2_ffn(nc, d, x, ident, ones_row):
    HT = 4
    with Stage(nc, "f2") as st:
        hT = st.sb("hT", [P, HT, N])
        w = st.sb("w", [P, NT, 8])
        w1, b1, wg = st.sb("w1", [P, 512]), st.sb("b1", [P, HT]), st.sb("wg", [P, HT * 8])
        bg, wd, bd = st.sb("bg", [1, 8]), st.sb("wd", [P, HT, 8 * C]), st.sb("bd", [1, 8 * C])
        load(nc, "f2l", [(w1[:, :], d["L2f_W1"]), (b1[:, :], d["L2f_b1"]), (wg[:, :], d["L2f_Wg"]),
                         (bg[:, :], d["L2f_bg"]), (flat(wd[:, :, :]), d["L2f_Wd"]), (bd[:, :], d["L2f_bd"])])
        with Stage(nc, "f2a") as s1:
            xn, xT = s1.sb("xn", [P, NT, C]), s1.sb("xT", [P, N])
            norm(nc, "f2n", x, xn, xT, ident, 1e-5)
            for k in range(HT):
                project_T(nc, f"f2h{k}", hT[:, k, :], [(w1[:, k * P:(k + 1) * P], xT)], ACT.Gelu, b1[:, k:k + 1])
        gate(nc, "f2g", w[:, :, :], [(hT[:, k, :], wg[:, k * 8:(k + 1) * 8]) for k in range(HT)], ones_row,
             [bg[:, :]], "top1")
        routed_add(nc, "f2r", x, hT, w[:, :, :], wd, bd[:, :], ones_row, HT)


def block3_graph(nc, d, x, ident, ones_row):
    with Stage(nc, "g3") as st:
        xn, aT = st.sb("xn", [P, NT, C]), st.sb("aT", [P, N])
        ev, t = st.sb("ev", [P, NT]), st.sb("t", [P, 1])
        load(nc, "g3l", [(ev[:, :], d["L3g_evals"]), (t[:, :], d["L3g_t"])])
        norm(nc, "g3n", x, xn, None, ident, 1e-5)
        with Stage(nc, "g3e") as s1:
            step, e = s1.sem("step"), s1.sem("e")
            with nc.Block() as block:
                @block.vector
                def _(dve):
                    chain = Chain(dve, step)
                    chain.step(dve.tensor_scalar(t[:, :], t[:, :], 1e-8, None, ALU.max))
                    dve.tensor_scalar(ev[:, :], ev[:, :], t[:, :], None, ALU.mult).then_inc(e, 1)

                @block.scalar
                def _(act):
                    act.wait_ge(e, 1)
                    act.activation(ev[:, :], ev[:, :], ACT.Exp, scale=-1.0)
        aggregate(nc, "g3a", d["adj_n"], xn, aT)

        def filtered(dve, chain, k, bank):
            s = slice(k * TPC, (k + 1) * TPC)
            chain.step(dve.tensor_tensor(xn[:, s, :], bank, over(ev[:, s], C), ALU.mult))
        to_nodes(nc, "g3b", aT, ident, filtered)
        aggregate(nc, "g3c", d["adj_t"], xn, aT)
        add_T(nc, "g3d", x, aT, ident)


def block3_ffn(nc, d, x, ident, ones_row, sel):
    with Stage(nc, "f3") as st:
        xn, xT, outT = st.sb("xn", [P, NT, C]), st.sb("xT", [P, N]), st.sb("outT", [P, N])
        w, wT = st.sb("w", [P, NT, 8]), st.sb("wT", [8, N])
        wg, bg, bb = st.sb("wg", [P, 8]), st.sb("bg", [1, 8]), st.sb("bb", [1, 8])
        w1, b1, w2, b2 = st.sb("w1", [P, 2048]), st.sb("b1", [P, 16]), st.sb("w2", [P, 16 * C]), st.sb("b2", [8, C])
        load(nc, "f3l", [(wg[:, :], d["L3f_Wg"]), (bg[:, :], d["L3f_bg"]), (bb[:, :], d["L3f_bias"]),
                         (w1[:, :], d["L3f_W1"]), (b1[:, :], d["L3f_b1"]), (w2[:, :], d["L3f_W2"]), (b2[:, :], d["L3f_b2"])])
        norm(nc, "f3n", x, xn, xT, ident, 1e-5)
        gate(nc, "f3g", w[:, :, :], [(xT, wg[:, :])], ones_row, [bg[:, :], bb[:, :]], "softmax2")
        transpose_gates(nc, "f3t", w, wT, ident)
        experts(nc, "f3e", xT, wT, sel, w1, None, b1, w2, b2[:, :], outT, (128, 128), ACT.Relu)
        add_T(nc, "f3x", x, outT, ident)


def adj_ffn_network(nc, d, out, first=0, last=8):
    with Stage(nc, "net") as st:
        x = st.sb("x", [P, NT, C])
        ident = st.sb("ident", [P, P])
        ones = st.sb("ones", [1, P])
        sel = st.sb("sel", [16, 16 * P])
        rowsum, edge = st.sb("rowsum", [P, NT]), st.sb("edge", [P, NT])
        d = dict(d, rowsum=rowsum, edge=edge)
        ident_, ones_row = ident[:, :], ones[:, :]
        make_identity(nc, ident_, ones_row)
        load(nc, "in", [(flat(x[:, :, :]), d["x"]), (sel[:, :], d["sel"])])
        if first <= 2:
            row_sums(nc, "rs", d["adj_n"], d["adj_t"], rowsum, edge)
        stages = [lambda: block0(nc, d, x, ident_, ones_row),
                  lambda: None,
                  lambda: block1_graph(nc, d, x, ident_, ones_row),
                  lambda: block1_ffn(nc, d, x, ident_, ones_row, sel),
                  lambda: block2_graph(nc, d, x, ident_, ones_row, sel),
                  lambda: block2_ffn(nc, d, x, ident_, ones_row),
                  lambda: block3_graph(nc, d, x, ident_, ones_row),
                  lambda: block3_ffn(nc, d, x, ident_, ones_row, sel[0:8, :])]
        for stage in stages[first:last]:
            stage()
        with Stage(nc, "out") as s1:
            stored = s1.sem("stored")
            with nc.Block() as block:
                @block.sync
                def _(sp):
                    sp.dma_start(out, flat(x[:, :, :])).then_inc(stored, 16)
                    sp.wait_ge(stored, 16)



def layouts(i):
    f = np.float32
    a = {k: np.asarray(v) for k, v in i.items()}
    row = lambda v: v.reshape(1, -1)
    col = lambda v, n: v.reshape(n, P).T
    allp = lambda v: np.broadcast_to(v.reshape(1, -1), (P, v.size))
    nodes = lambda v: v.reshape(NT, P, -1).transpose(1, 0, 2).reshape(P, -1)
    adj = a["adj"]
    rot = np.concatenate([np.concatenate([np.arange(16, 32), np.arange(0, 16)]) + 32 * h for h in range(4)])
    wqT, wkT = a["L1_ffn_wq"].T, a["L1_ffn_wk"].T
    sizes = (128, 128, 85)
    w2 = a["L1_ffn_w2"].transpose(0, 2, 1)
    w2t = np.zeros((P, 24, C), f)
    for e in range(8):
        for h, m in enumerate(sizes):
            w2t[0:m, e * 3 + h] = w2[e, h * P:h * P + m]
    inv_freq = 1.0 / 10000.0 ** (np.arange(0, 32, 2, dtype=f) / 32)
    freqs = np.outer(np.arange(N, dtype=f), inv_freq)
    emb = np.concatenate([freqs, freqs], axis=-1)
    sign = np.concatenate([-np.ones(16, f), np.ones(16, f)])
    cos = np.tile(np.cos(emb).T, (4, 1))
    sin = np.tile((np.sin(emb) * sign).T, (4, 1))
    q, c = np.arange(P)[:, None], np.arange(CH)[None, :]
    mask = np.concatenate([np.where(c <= q + P * j, 0.0, -1e30) for j in range(TPC)], axis=1)
    sel = np.kron(np.eye(16), np.ones((1, P)))
    halves = lambda v: v.reshape(2, P, -1).transpose(1, 0, 2).reshape(P, -1)
    out = dict(
        x=nodes(a["x"]),
        adj_n=adj.reshape(NQ, JT, P, NCH, CH).transpose(3, 0, 2, 1, 4),
        adj_t=adj.reshape(NCH, CH, NQ, JT, P).transpose(0, 2, 4, 3, 1),
        sel=sel, cos=cos, sin=sin, mask=mask,
        L0_W1=a["L0_gnn_W1"].T, L0_W2=a["L0_gnn_W2"].T, L0_W3=a["L0_gnn_W3"].T,
        L0_U1=a["L0_gnn_U1"].transpose(2, 0, 1).reshape(C, -1),
        L0_U2=a["L0_gnn_U2"].transpose(2, 0, 1).reshape(C, -1),
        L0_g=allp(a["L0_gnn_ln_g"]), L0_b=allp(a["L0_gnn_ln_b"]),
        L0f_w=a["L0_ffn_weight"].T, L0f_b=row(a["L0_ffn_bias"]),
        L1g_w=np.concatenate([a["L1_gnn_weight"][0:C], a["L1_gnn_weight"][C:2 * C]], axis=1),
        L1g_wc=allp(a["L1_gnn_weight"][2 * C]), L1g_b=row(a["L1_gnn_bias"]),
        L1f_ln=np.stack([a["L1_ffn_ln1_w"], a["L1_ffn_ln2_w"]], axis=1),
        L1f_wq=np.concatenate([wqT, wqT[:, rot]], axis=1),
        L1f_wk=np.concatenate([wkT, wkT[:, rot[:64]]], axis=1),
        L1f_wv=a["L1_ffn_wv"].T, L1f_wo=a["L1_ffn_wo"].T, L1f_wr=a["L1_ffn_router_w"].T,
        L1f_w1=a["L1_ffn_w1"].reshape(-1, C).T, L1f_w3=a["L1_ffn_w3"].reshape(-1, C).T,
        L1f_w2=w2t.reshape(P, -1),
        L2g_gcn=a["L2_gnn_gcn_w"],
        L2g_cols=np.stack([a["L2_gnn_gcn_b"], a["L2_gnn_ln_g"], a["L2_gnn_ln_b"]], axis=1),
        L2g_w_in=a["L2_gnn_w_in"], L2g_conv=halves(a["L2_gnn_conv_w"]), L2g_conv_b=col(a["L2_gnn_conv_b"], 2),
        L2g_w_xp=halves(a["L2_gnn_w_xp"]), L2g_w_dt=a["L2_gnn_w_dt"], L2g_b_dt=col(a["L2_gnn_b_dt"], 2),
        L2g_A=halves(a["L2_gnn_A_log"]), L2g_D=col(a["L2_gnn_D_skip"], 2), L2g_w_out=halves(a["L2_gnn_w_out"]),
        L2f_W1=a["L2_ffn_W1"], L2f_b1=col(a["L2_ffn_b1"], 4),
        L2f_Wg=a["L2_ffn_Wg"].reshape(4, P, 8).transpose(1, 0, 2).reshape(P, -1), L2f_bg=row(a["L2_ffn_bg"]),
        L2f_Wd=a["L2_ffn_Wd"].reshape(8, 4, P, C).transpose(2, 1, 0, 3).reshape(P, -1), L2f_bd=row(a["L2_ffn_bd"]),
        L3g_evals=nodes(a["L3_gnn_evals"]), L3g_t=allp(a["L3_gnn_t"]),
        L3f_Wg=a["L3_ffn_Wg"], L3f_bg=row(a["L3_ffn_bg"]), L3f_bias=row(a["L3_ffn_bias"]),
        L3f_W1=a["L3_ffn_W1"].transpose(1, 0, 2).reshape(C, -1),
        L3f_b1=a["L3_ffn_b1"].reshape(16, P).T,
        L3f_W2=a["L3_ffn_W2"].reshape(16, P, C).transpose(1, 0, 2).reshape(P, -1), L3f_b2=a["L3_ffn_b2"],
    )
    out = {k: np.ascontiguousarray(v, dtype=f) for k, v in out.items()}
    for k in ("adj_n", "adj_t"):
        out[k] = out[k].reshape(NCH, NQ, P, JT, CH)
    return out


def program(nc, arrays, first=0, last=8):
    d = {k: nc.dram_tensor(f"in_{k}", v.shape, F32, kind="ExternalInput").ap() for k, v in arrays.items()}
    d["q_dram"] = nc.dram_tensor("q_dram", (32, NCH, 2, TPC, 2, P), F32, kind="Internal").ap()
    out = nc.dram_tensor("out", (P, NT * C), F32, kind="ExternalOutput").ap()
    adj_ffn_network(nc, d, out, first, last)


def kernel(**inputs):
    import concourse.bacc as bacc
    from concourse.bass_utils import run_bass_kernel_spmd

    nc = bacc.Bacc("TRN2", target_bir_lowering=False, num_devices=1)
    arrays = layouts(inputs)
    program(nc, arrays)
    r = run_bass_kernel_spmd(nc, [{f"in_{k}": v for k, v in arrays.items()}], core_ids=[0])
    return r.results[0]["out"].reshape(P, NT, C).transpose(1, 0, 2).reshape(N, C)
```
